# Optimizing a Trainium2 kernel written in Bass

```python
import numpy as np
import jax
import jax.numpy as jnp

def _softmax(x, axis=-1):
    return jax.nn.softmax(x, axis=axis)

def _gelu(x):
    return jax.nn.gelu(x, approximate=True)

def _silu(x):
    return jax.nn.silu(x)

def _sigmoid(x):
    return jax.nn.sigmoid(x)

def _layernorm(x, axis=-1, eps=1e-05):
    m = jnp.mean(x, axis=axis, keepdims=True)
    v = jnp.var(x, axis=axis, keepdims=True)
    return (x - m) / jnp.sqrt(v + eps)

def _scatter_add(tgt, idx, src, axis=0):
    return tgt.at[idx].add(src)

def _segment_sum(src, seg, n):
    return jax.ops.segment_sum(src, seg, n)
kernel_name = 'mk_decoder_preln_d1_seqx_r8_994773'

def setup_inputs(seed: int=0):
    np.random.seed(seed)
    _w = jnp.asarray

    def _rec_inputs():
        import jax
        import jax.numpy as jnp
        _rk = jax.random.key(seed)
        x = -0.0002928 + 1 * jax.random.normal(jax.random.fold_in(_rk, 1), (32, 128, 128), jnp.float32)
        _lenS = 128 - jax.random.randint(jax.random.fold_in(_rk, 7), (32,), 0, max(1, 128 // 4) + 1, jnp.int32)
        _lenS2 = 128 - jax.random.randint(jax.random.fold_in(_rk, 8), (32,), 0, max(1, 128 // 4) + 1, jnp.int32)
        _ctx_1024P = jax.random.normal(jax.random.fold_in(_rk, 11), (32, 16, 128), jnp.float32)
        _ctx_1024c = jax.random.dirichlet(jax.random.fold_in(_rk, 511), 0.3 * jnp.ones((16,), jnp.float32), (32, 128))
        _ctx_1024t = jnp.einsum('bsk,bkd->bsd', _ctx_1024c, _ctx_1024P)
        _ctx_1024t = _ctx_1024t * jax.lax.rsqrt(jnp.mean(jnp.square(_ctx_1024t)) + 1e-12) * 0.953939
        ctx_1024 = -1.39393e-06 + 0.999914 * (_ctx_1024t + 0.3 * jax.random.normal(jax.random.fold_in(_rk, 611), (32, 128, 128), jnp.float32))
        return (x, ctx_1024)
    x, ctx_1024 = _rec_inputs()

    def _L0_attn_setup():
        import jax, jax.numpy as jnp
        import numpy as np
        N_HEAD = 16
        WINDOW = 128
        CAUSAL = False

        def _window_attention(x, w_in, b_in, w_out, b_out):
            B, T, D = x.shape
            H = N_HEAD
            hd = D // H
            scale = 1.0 / jnp.sqrt(jnp.float32(hd))
            qkv = jnp.einsum('btd,ed->bte', x, w_in) + b_in
            q, k, v = jnp.split(qkv, 3, axis=-1)
            q = q.reshape(B, T, H, hd).transpose(0, 2, 1, 3)
            k = k.reshape(B, T, H, hd).transpose(0, 2, 1, 3)
            v = v.reshape(B, T, H, hd).transpose(0, 2, 1, 3)
            scores = jnp.einsum('bhqd,bhkd->bhqk', q, k) * scale
            idx = jnp.arange(T)
            diff = idx[:, None] - idx[None, :]
            if CAUSAL:
                allowed = (diff >= 0) & (diff <= WINDOW)
            else:
                allowed = jnp.abs(diff) <= WINDOW
            NEG = jnp.float32(-1e+30)
            scores = jnp.where(allowed[None, None, :, :], scores, NEG)
            attn = jax.nn.softmax(scores, axis=-1)
            ctx = jnp.einsum('bhqk,bhkd->bhqd', attn, v)
            ctx = ctx.transpose(0, 2, 1, 3).reshape(B, T, D)
            out = jnp.einsum('btd,ed->bte', ctx, w_out) + b_out
            return x + out
        key = jax.random.key(seed)
        ks = jax.random.split(key, 5)
        B, T, D = (1, 512, 128)
        x = jax.random.normal(ks[0], (B, T, D), dtype=jnp.float32)
        w_in = jax.random.normal(ks[1], (3 * D, D), dtype=jnp.float32) * 0.02
        b_in = jax.random.normal(ks[2], (3 * D,), dtype=jnp.float32) * 0.02
        w_out = jax.random.normal(ks[3], (D, D), dtype=jnp.float32) * 0.02
        b_out = jax.random.normal(ks[4], (D,), dtype=jnp.float32) * 0.02
        return {'x': x, 'w_in': w_in, 'b_in': b_in, 'w_out': w_out, 'b_out': b_out}
    _L0_attn_all = _L0_attn_setup()
    _L0_attn_in = {k: v for k, v in _L0_attn_all.items() if k in ('w_in', 'b_in', 'w_out', 'b_out')}
    del _L0_attn_all

    def _L0_xattn_setup():
        import jax, jax.numpy as jnp
        import numpy as np
        B, L, DIM = (2, 256, 128)
        H, DH, W = (16, 64, 32)
        ROPE_BASE = 10000.0

        def _rope(x):
            l, d = (x.shape[1], x.shape[3])
            freqs = 1.0 / ROPE_BASE ** (jnp.arange(0, d, 2, dtype=jnp.float32) / d)
            ang = jnp.arange(l, dtype=jnp.float32)[:, None] * freqs[None, :]
            cos = jnp.cos(ang)[None, :, None, :].astype(x.dtype)
            sin = jnp.sin(ang)[None, :, None, :].astype(x.dtype)
            xe, xo = (x[..., 0::2], x[..., 1::2])
            ye = xe * cos - xo * sin
            yo = xe * sin + xo * cos
            return jnp.stack([ye, yo], axis=-1).reshape(x.shape)
        key = jax.random.key(seed)
        ks = jax.random.split(key, 7)
        sh = (B, L, DIM)
        return {'q': jax.random.normal(ks[0], sh, jnp.float32), 'k': jax.random.normal(ks[1], sh, jnp.float32), 'v': jax.random.normal(ks[2], sh, jnp.float32), 'wq': jax.random.normal(ks[3], (H * DH, DIM), jnp.float32) * 0.02, 'wk': jax.random.normal(ks[4], (H * DH, DIM), jnp.float32) * 0.02, 'wv': jax.random.normal(ks[5], (H * DH, DIM), jnp.float32) * 0.02, 'wo': jax.random.normal(ks[6], (DIM, H * DH), jnp.float32) * 0.02}
    _L0_xattn_all = _L0_xattn_setup()
    _L0_xattn_in = {k: v for k, v in _L0_xattn_all.items() if k in ('wq', 'wk', 'wv', 'wo')}
    del _L0_xattn_all

    def _L0_ffn_setup():
        import jax, jax.numpy as jnp
        import numpy as np
        B, T, C, H, E = (1, 32, 128, 256, 8)
        STD = 0.02
        key = jax.random.key(seed)
        ks = jax.random.split(key, 8)
        f32 = jnp.float32
        return {'x': jax.random.normal(ks[0], (B, T, C), f32), 'up': jax.random.normal(ks[1], (E, H, C), f32) * STD, 'gate': jax.random.normal(ks[2], (E, H, C), f32) * STD, 'down': jax.random.normal(ks[3], (E, C, H), f32) * STD, 'router': jax.random.normal(ks[4], (E, C), f32) * STD, 'w_up_s': jax.random.normal(ks[5], (H, C), f32) * STD, 'w_gate_s': jax.random.normal(ks[6], (H, C), f32) * STD, 'w_down_s': jax.random.normal(ks[7], (C, H), f32) * STD}
    _L0_ffn_all = _L0_ffn_setup()
    _L0_ffn_in = {k: v for k, v in _L0_ffn_all.items() if k in ('up', 'gate', 'down', 'router', 'w_up_s', 'w_gate_s', 'w_down_s')}
    del _L0_ffn_all
    return {'x': x, 'ctx_1024': ctx_1024, 'L0_attn_w_in': _L0_attn_in['w_in'], 'L0_attn_b_in': _L0_attn_in['b_in'], 'L0_attn_w_out': _L0_attn_in['w_out'], 'L0_attn_b_out': _L0_attn_in['b_out'], 'L0_xattn_wq': _L0_xattn_in['wq'], 'L0_xattn_wk': _L0_xattn_in['wk'], 'L0_xattn_wv': _L0_xattn_in['wv'], 'L0_xattn_wo': _L0_xattn_in['wo'], 'L0_ffn_up': _L0_ffn_in['up'], 'L0_ffn_gate': _L0_ffn_in['gate'], 'L0_ffn_down': _L0_ffn_in['down'], 'L0_ffn_router': _L0_ffn_in['router'], 'L0_ffn_w_up_s': _L0_ffn_in['w_up_s'], 'L0_ffn_w_gate_s': _L0_ffn_in['w_gate_s'], 'L0_ffn_w_down_s': _L0_ffn_in['w_down_s']}

def reference(x, ctx_1024, L0_attn_w_in, L0_attn_b_in, L0_attn_w_out, L0_attn_b_out, L0_xattn_wq, L0_xattn_wk, L0_xattn_wv, L0_xattn_wo, L0_ffn_up, L0_ffn_gate, L0_ffn_down, L0_ffn_router, L0_ffn_w_up_s, L0_ffn_w_gate_s, L0_ffn_w_down_s):
    import jax
    import jax.numpy as jnp

    def _L0_attn_ref(x, w_in, b_in, w_out, b_out):
        import jax, jax.numpy as jnp
        import numpy as np
        N_HEAD = 16
        WINDOW = 128
        CAUSAL = False

        def _window_attention(x, w_in, b_in, w_out, b_out):
            B, T, D = x.shape
            H = N_HEAD
            hd = D // H
            scale = 1.0 / jnp.sqrt(jnp.float32(hd))
            qkv = jnp.einsum('btd,ed->bte', x, w_in) + b_in
            q, k, v = jnp.split(qkv, 3, axis=-1)
            q = q.reshape(B, T, H, hd).transpose(0, 2, 1, 3)
            k = k.reshape(B, T, H, hd).transpose(0, 2, 1, 3)
            v = v.reshape(B, T, H, hd).transpose(0, 2, 1, 3)
            scores = jnp.einsum('bhqd,bhkd->bhqk', q, k) * scale
            idx = jnp.arange(T)
            diff = idx[:, None] - idx[None, :]
            if CAUSAL:
                allowed = (diff >= 0) & (diff <= WINDOW)
            else:
                allowed = jnp.abs(diff) <= WINDOW
            NEG = jnp.float32(-1e+30)
            scores = jnp.where(allowed[None, None, :, :], scores, NEG)
            attn = jax.nn.softmax(scores, axis=-1)
            ctx = jnp.einsum('bhqk,bhkd->bhqd', attn, v)
            ctx = ctx.transpose(0, 2, 1, 3).reshape(B, T, D)
            out = jnp.einsum('btd,ed->bte', ctx, w_out) + b_out
            return x + out
        return _window_attention(x, w_in, b_in, w_out, b_out)

    def _L0_xattn_ref(q, k, v, wq, wk, wv, wo):
        import jax, jax.numpy as jnp
        import numpy as np
        B, L, DIM = (2, 256, 128)
        H, DH, W = (16, 64, 32)
        ROPE_BASE = 10000.0

        def _rope(x):
            l, d = (x.shape[1], x.shape[3])
            freqs = 1.0 / ROPE_BASE ** (jnp.arange(0, d, 2, dtype=jnp.float32) / d)
            ang = jnp.arange(l, dtype=jnp.float32)[:, None] * freqs[None, :]
            cos = jnp.cos(ang)[None, :, None, :].astype(x.dtype)
            sin = jnp.sin(ang)[None, :, None, :].astype(x.dtype)
            xe, xo = (x[..., 0::2], x[..., 1::2])
            ye = xe * cos - xo * sin
            yo = xe * sin + xo * cos
            return jnp.stack([ye, yo], axis=-1).reshape(x.shape)
        b, l, _ = q.shape
        qh = (q @ wq.T).reshape(b, l, H, DH)
        kh = (k @ wk.T).reshape(b, l, H, DH)
        vh = (v @ wv.T).reshape(b, l, H, DH).transpose(0, 2, 1, 3)
        qh = _rope(qh).transpose(0, 2, 1, 3)
        kh = _rope(kh).transpose(0, 2, 1, 3)
        scores = jnp.einsum('bhqd,bhkd->bhqk', qh, kh) * DH ** (-0.5)
        i = jnp.arange(l)[:, None]
        j = jnp.arange(l)[None, :]
        window_mask = (j <= i) & (j >= i - W)
        scores = jnp.where(window_mask, scores, -1e+30)
        probs = jax.nn.softmax(scores, axis=-1)
        out = jnp.einsum('bhqk,bhkd->bhqd', probs, vh)
        out = out.transpose(0, 2, 1, 3).reshape(b, l, H * DH)
        return out @ wo.T

    def _L0_ffn_ref(x, up, gate, down, router, w_up_s, w_gate_s, w_down_s):
        import jax, jax.numpy as jnp
        import numpy as np
        B, T, C, H, E = (1, 32, 128, 256, 8)
        STD = 0.02
        b, t, c = x.shape
        x_ = x.reshape(b * t, c)
        logits = x_ @ router.T
        idx = jnp.argmax(logits, axis=-1)
        onehot = jax.nn.one_hot(idx, router.shape[0], dtype=x.dtype)
        u = jnp.einsum('bc,ehc->ebh', x_, up)
        g = jnp.einsum('bc,ehc->ebh', x_, gate)
        h = jax.nn.silu(g) * u
        ye = jnp.einsum('ebh,ech->ebc', h, down)
        y = jnp.einsum('ebc,be->bc', ye, onehot)
        ys = jax.nn.silu(x_ @ w_gate_s.T) * (x_ @ w_up_s.T) @ w_down_s.T
        return (y + ys).reshape(b, t, c)
    x = x + _L0_attn_ref(_layernorm(x, axis=-1), L0_attn_w_in, L0_attn_b_in, L0_attn_w_out, L0_attn_b_out)
    x = x + _L0_xattn_ref(_layernorm(x, axis=-1), ctx_1024, ctx_1024, L0_xattn_wq, L0_xattn_wk, L0_xattn_wv, L0_xattn_wo)
    x = x + _L0_ffn_ref(_layernorm(x, axis=-1), L0_ffn_up, L0_ffn_gate, L0_ffn_down, L0_ffn_router, L0_ffn_w_up_s, L0_ffn_w_gate_s, L0_ffn_w_down_s)
    return x

_drawn_inputs = setup_inputs


def setup_inputs(seed=0):
    import zlib

    import numpy as np

    out = dict(_drawn_inputs(seed))
    spreads = {}
    factors = {'L0_attn_w_in': 8.0,
     'L0_attn_b_in': 8.0,
     'L0_attn_w_out': 8.0,
     'L0_attn_b_out': 5.525,
     'L0_xattn_wq': 8.0,
     'L0_xattn_wk': 8.0,
     'L0_ffn_up': 8.0,
     'L0_ffn_gate': 8.0,
     'L0_ffn_down': 8.0,
     'L0_ffn_router': 8.0,
     'L0_ffn_w_up_s': 8.0,
     'L0_ffn_w_gate_s': 8.0,
     'L0_ffn_w_down_s': 8.0}
    for name, (base, spread) in spreads.items():
        noise = np.random.default_rng([zlib.crc32(name.encode()), seed]).standard_normal(out[name].shape)
        drawn = base * np.exp(spread * noise) if base else spread * noise
        out[name] = jnp.asarray(drawn.astype(out[name].dtype))
    for name, factor in factors.items():
        out[name] = (out[name] * factor).astype(out[name].dtype)
    return out
```

```python
from contextlib import ExitStack

import concourse.bass as bass
from concourse import mybir

F32 = mybir.dt.float32
BF16 = mybir.dt.bfloat16
U32 = mybir.dt.uint32
ALU = mybir.AluOpType
ACT = mybir.ActivationFunctionType
AX = mybir.AxisListType

NB = 32
NH = 16
NE = 8
S_SELF = float(8.0 ** -0.5)
S_X = 0.125


def on(*args, **kw):
    return args, kw


def op_activation(e, *x, **k):
    return e.activation(*x, **k)


def op_bn_aggr(e, *x, **k):
    return e.bn_aggr(*x, **k)


def op_bn_stats(e, *x, **k):
    return e.bn_stats(*x, **k)


def op_matmul(e, *x, **k):
    return e.matmul(*x, **k)


def op_max(e, *x, **k):
    return e.max(*x, **k)


def op_max_index(e, *x, **k):
    return e.max_index(*x, **k)


def op_memset(e, *x, **k):
    return e.memset(*x, **k)


def op_reciprocal(e, *x, **k):
    return e.reciprocal(*x, **k)


def op_scalar_tensor_tensor(e, *x, **k):
    return e.scalar_tensor_tensor(*x, **k)


def op_tensor_copy(e, *x, **k):
    return e.tensor_copy(*x, **k)


def op_tensor_reduce(e, *x, **k):
    return e.tensor_reduce(*x, **k)


def op_tensor_scalar(e, *x, **k):
    return e.tensor_scalar(*x, **k)


def op_tensor_tensor(e, *x, **k):
    return e.tensor_tensor(*x, **k)


def op_transpose(e, *x, **k):
    return e.transpose(*x, **k)


class Queue:

    def __init__(self, sem):
        self.sem, self.n, self.ops, self.seen = sem, 0, [], {}

    def wait(self, *toks):
        for t in toks:
            if t is None:
                continue
            if isinstance(t, list):
                self.wait(*t)
                continue
            sem, val = t
            if self.seen.get(id(sem), 0) < val:
                self.seen[id(sem)] = val
                self.ops.append(lambda e, sem=sem, val=val: e.wait_ge(sem, val))

    def do(self, fn, what, *toks, sig=True):
        self.wait(*toks)
        if not sig:
            self.ops.append(lambda e: fn(e, *what[0], **what[1]))
            return None
        self.n += 1
        self.ops.append(lambda e: fn(e, *what[0], **what[1]).then_inc(self.sem, 1))
        return (self.sem, self.n)

    def dma(self, stream, out, in_, *toks):
        self.wait(*toks)
        stream[1] += 16
        self.ops.append(lambda e: e.dma_start(out, in_).then_inc(stream[0], 16))
        return (stream[0], stream[1])


class Slot:
    def __init__(self, ap):
        self.ap, self.free, self.held = ap, [], False

    def release(self, *toks):
        self.free = list(toks)
        self.held = False


class Ring:

    def __init__(self, aps):
        self.slots, self.at = [Slot(a) for a in aps], 0

    def take(self):
        s = self.slots[self.at % len(self.slots)]
        self.at += 1
        assert not s.held
        s.held = True
        return s, s.free


def build(nc, A):
    ctx = ExitStack()
    with ctx:
        def sb(name, shape, dt=F32):
            return ctx.enter_context(nc.sbuf_tensor(name, shape, dt))

        def sem(name):
            return ctx.enter_context(nc.semaphore(name))

        def stream(name):
            return [sem(name), 0]

        pe, dve, act, pool, sp = (Queue(sem(f"q_{n}")) for n in ("pe", "dve", "act", "pool", "sp"))

        P = ctx.enter_context(nc.psum_tensor("P", [128, 8, 512], F32))
        bank = [P[:, k, :] for k in range(8)]
        rA, rS, rC, rX = Ring(bank[0:2]), Ring(bank[2:4]), Ring(bank[4:6]), Ring(bank[6:8])

        ident = sb("ident", [128, 128])
        identb = sb("identb", [128, 128], BF16)
        cos = sb("cos", [128, 128])
        sin = sb("sin", [128, 128])
        mask = sb("mask", [128, 512], BF16)
        iota = sb("iota", [128, 8])
        nhalf = sb("nhalf", [128, 1])
        bqk = sb("bqk", [128, 2])
        bv = sb("bv", [128, 128])
        bo = sb("bo", [128, 128])
        winT = sb("winT", [128, 384])
        woutT = sb("woutT", [128, 128])
        wqT = sb("wqT", [128, 8, 128])
        wqJ = sb("wqJ", [128, 8, 128])
        wkT = sb("wkT", [128, 8, 128])
        wkJ = sb("wkJ", [128, 8, 128])
        wvT = sb("wvT", [128, 8, 128])
        woT = sb("woT", [128, 8, 128])
        rtT = sb("rtT", [128, 8])
        wgu = sb("wgu", [128, NE + 1, 512])
        wd = sb("wd", [128, NE + 1, 2, 128])
        stage = Ring([sb(f"stage{i}", [128, 8, 128]) for i in range(4)])

        def staged(parts):
            s, free = stage.take()
            st = stage_stream[(stage.at - 1) % 4]
            for dst, src in parts:
                t = sp.dma(st, dst(s.ap), src, *free)
            return s, t

        stage_stream = [stream(f"d_st{i}") for i in range(4)]
        d_c = stream("d_c")
        for dst, src in ((ident, A["ident"]), (cos, A["cos"]), (sin, A["sin"]), (iota, A["iota"]),
                         (bqk, A["bqk"]), (bv, A["bvb"]),
                         (bo, A["bob"])):
            t_c = sp.dma(d_c, dst[:, :], src)
        t_idb = dve.do(op_tensor_copy, on(identb[:, :], ident[:, :]), t_c)
        t_nh = pool.do(op_memset, on(nhalf[:, :], -0.5))
        maskf, free = stage.take()
        st = stage_stream[(stage.at - 1) % 4]
        t = sp.dma(st, maskf.ap[:, 0:4, :], A["mask"].rearrange("p (a n) -> p a n", a=4))
        t_mask = dve.do(op_tensor_copy, on(mask[:, :].rearrange("p (a n) -> p a n", a=4), maskf.ap[:, 0:4, :]), t)
        maskf.release(t_mask)

        flip = [0]

        def evac(out, in_, *toks):
            flip[0] ^= 1
            if flip[0]:
                return dve.do(op_tensor_copy, on(out, in_), *toks)
            return act.do(op_activation, on(out, in_, ACT.Copy), *toks)

        def turn(s, t, n, outs, rows=128):
            done = []
            for b0 in range(0, n, 4):
                k = min(4, n - b0)
                p, pf = rA.take()
                for j in range(k):
                    tt = pe.do(op_transpose, on(p.ap[:, j * 128:j * 128 + rows],
                                                          s.ap[0:rows, b0 + j, :], ident[0:rows, 0:rows]),
                               t, t_c, *pf, sig=(j == k - 1))
                    pf = []
                ts = []
                for n_, (o, i) in enumerate(outs(b0, k, p.ap)):
                    if n_:
                        flip[0] ^= 1
                    ts.append(evac(o, i, tt))
                p.release(*ts)
                done += ts
                last = tt
            s.release(last)
            return done

        def v3(ap, k):
            return ap[:, 0:k * 128].rearrange("p (a n) -> p a n", a=k)

        W = {}

        def setup_a():
            s, t = staged([(lambda a: a[:, 0:3, :], A["L0_attn_w_in"].rearrange("(a p) d -> p a d", p=128)),
                           (lambda a: a[:, 3, :], A["L0_attn_w_out"])])
            W["a"] = turn(s, t, 4, lambda b0, k, p: [
                (winT[:, 0:256].rearrange("p (j d h) -> p j h d", j=2, d=8),
                 p[:, 0:256].rearrange("p (j h d) -> p j h d", j=2, d=8)),
                (winT[:, 256:384], p[:, 256:384]), (woutT[:, :], p[:, 384:512])])
            yield
            for name, dst, dj in (("L0_xattn_wk", wkT, wkJ), ("L0_xattn_wq", wqT, wqJ)):
                src = A[name].rearrange("(t h f e) d -> h e f t d", t=8, h=2, e=2)
                s, t = staged([(lambda a, q=2 * h + e: a[32 * q:32 * q + 32, :, :], src[h, e])
                               for h in range(2) for e in range(2)])

                def outs(b0, k, p, dst=dst, dj=dj):
                    pv = v3(p, 4)
                    o = [(dst[:, b0:b0 + 4, :], pv)]
                    for q in range(2):
                        o.append((dj[:, b0:b0 + 4, :].rearrange("p t (h e f) -> p t h e f", h=2, e=2)[:, :, :, q, :],
                                  pv.rearrange("p t (h e f) -> p t h e f", h=2, e=2)[:, :, :, 1 - q, :]))
                    return o
                W[name] = turn(s, t, 8, outs)
                yield
            s, t = staged([(lambda a: a[:, :, :], A["L0_xattn_wv"].rearrange("(t p) d -> p t d", p=128))])
            W["wv"] = turn(s, t, 8, lambda b0, k, p: [(wvT[:, b0:b0 + 4, :], v3(p, 4))])
            yield
            s, t = staged([(lambda a: a[:, :, :], A["L0_xattn_wo"].rearrange("o (t p) -> o t p", p=128))])
            W["wo"] = turn(s, t, 8, lambda b0, k, p: [(woT[:, b0:b0 + 4, :], v3(p, 4))])
            yield

        def setup_f():
            s, t = staged([(lambda a: a[0:8, 0, :], A["L0_ffn_router"])])
            W["rt"] = turn(s, t, 1, lambda b0, k, p: [(rtT[:, :], p[:, 0:8])], rows=8)
            yield
            W["f"] = []
            for half in range(2):
                for q, name in ((0, "L0_ffn_gate"), (1, "L0_ffn_up")):
                    src = A[name][4 * half:4 * half + 4].rearrange("e (t p) c -> p (e t) c", p=128)
                    s, t = staged([(lambda a: a[:, :, :], src)])
                    W["f"] += turn(s, t, 8, lambda b0, k, p, q=q, half=half: [
                        (wgu[:, 4 * half + b0 // 2:4 * half + b0 // 2 + 2, 256 * q:256 * q + 256],
                         p[:, :].rearrange("p (e n) -> p e n", e=2))])
                    yield
                src = A["L0_ffn_down"][4 * half:4 * half + 4].rearrange("e c (t h) -> c e t h", t=2)
                s, t = staged([(lambda a: a[:, :, :].rearrange("p (e t) h -> p e t h", t=2), src)])
                W["f"] += turn(s, t, 8, lambda b0, k, p, half=half: [
                    (wd[:, 4 * half + b0 // 2:4 * half + b0 // 2 + 2, :, :].rearrange("p e t n -> p (e t) n"), v3(p, 4))])
                yield
            s, t = staged([(lambda a: a[:, 0:2, :], A["L0_ffn_w_gate_s"].rearrange("(t p) c -> p t c", p=128)),
                           (lambda a: a[:, 2:4, :], A["L0_ffn_w_up_s"].rearrange("(t p) c -> p t c", p=128)),
                           (lambda a: a[:, 4:6, :], A["L0_ffn_w_down_s"].rearrange("c (t h) -> c t h", t=2))])

            def outs(b0, k, p):
                if b0 == 0:
                    return [(wgu[:, NE, :], p[:, :])]
                return [(wd[:, NE, :, :], v3(p, 2))]
            W["f"] += turn(s, t, 6, outs)
            yield

        xs = Ring([sb(f"x{i}", [128, 128]) for i in range(3)])
        d_x = [stream(f"d_x{i}") for i in range(3)]
        cs = Ring([sb(f"cx{i}", [128, 128]) for i in range(5)])
        d_cx = [stream(f"d_cx{i}") for i in range(5)]
        xab = Ring([sb(f"xab{i}", [128, 128]) for i in range(4)])
        arow = Ring([sb(f"arow{i}", [128, 128]) for i in range(2)])
        aT = Ring([sb(f"aT{i}", [128, 128]) for i in range(2)])
        qk = Ring([sb(f"qk{i}", [128, 2, 128]) for i in range(2)])
        res = Ring([sb(f"res{i}", [128, 2, 128]) for i in range(2)])
        parts = Ring([sb(f"parts{i}", [128, 2, 3, 128], BF16) for i in range(2)])
        d_sk = [stream(f"d_sk{i}") for i in range(2)]
        d_nm = [stream(f"d_nm{i}") for i in range(2)]
        d_zs = [stream(f"d_zs{i}") for i in range(2)]
        d_zn = [stream(f"d_zn{i}") for i in range(2)]
        vpad = Ring([sb(f"vpad{i}", [128, NH, 32]) for i in range(3)])
        QS = Ring([sb(f"QS{i}", [75, NH, 128], BF16) for i in range(2)])
        KS = [sb(f"KS{i}", [75, NH, 128], BF16) for i in range(2)]
        nm = Ring([sb(f"nm{i}", [128, 3, NH], BF16) for i in range(2)])
        nmf = [sb(f"nmf{i}", [128, 2, NH]) for i in range(2)]
        nmT = [sb(f"nmT{i}", [48, 128], BF16) for i in range(2)]
        PS = Ring([sb(f"PS{i}", [128, 4, 128]) for i in range(3)])
        oT = Ring([sb(f"oT{i}", [128, 512]) for i in range(2)])
        rs = Ring([sb(f"rs{i}", [128, NH]) for i in range(2)])
        cn = Ring([sb(f"cn{i}", [128, 128]) for i in range(2)])
        cnT = Ring([sb(f"cnT{i}", [128, 128]) for i in range(2)])
        x1 = Ring([sb(f"xi{i}", [128, 128]) for i in range(4)])
        lnr = Ring([sb(f"lnr{i}", [128, 128]) for i in range(3)])
        cT = Ring([sb(f"cT{i}", [128, 128]) for i in range(3)])
        cxT = Ring([sb(f"cxT{i}", [128, 128]) for i in range(2)])
        t12 = Ring([sb(f"t12_{i}", [128, 2, 4, 128]) for i in range(2)])
        rot = Ring([sb(f"rot{i}", [128, 2, 8, 128]) for i in range(2)])
        V = Ring([sb(f"V{i}", [128, NH, 64]) for i in range(2)])
        mxs = Ring([sb(f"mxs{i}", [128, 16]) for i in range(2)])
        mx = Ring([sb(f"mx{i}", [128, 16]) for i in range(8)])
        PX = Ring([sb(f"PX{i}", [128, 4, 128]) for i in range(2)])
        PN = Ring([sb(f"PN{i}", [128, 4, 128]) for i in range(2)])
        PT = Ring([sb(f"PT{i}", [128, 4, 128]) for i in range(3)])
        oX = Ring([sb(f"oX{i}", [128, 4, 128]) for i in range(3)])
        x2 = Ring([sb(f"xj{i}", [128, 128]) for i in range(3)])
        eT = Ring([sb(f"eT{i}", [128, 128]) for i in range(2)])
        st6 = Ring([sb(f"st6_{i}", [128, 12]) for i in range(6)])
        lg = Ring([sb(f"lg{i}", [128, 40]) for i in range(2)])
        lgu = [sb(f"lgu{i}", [128, 8], U32) for i in range(2)]
        th = Ring([sb(f"th{i}", [128, 2, 256]) for i in range(2)])
        hb = Ring([sb(f"hb{i}", [128, 2, 128]) for i in range(2)])
        hT = Ring([sb(f"hT{i}", [128, NE + 1, 2, 128]) for i in range(1)])
        xo = Ring([sb(f"xo{i}", [128, 128]) for i in range(2)])
        d_o = [stream(f"d_o{i}") for i in range(2)]

        t_vp = []
        for s in vpad.slots:
            a = dve.do(op_memset, on(s.ap[:, :, :], 0.0))
            t_vp.append(dve.do(op_memset, on(s.ap[:, :, 8:9], 1.0), a))
        t_ks = [dve.do(op_memset, on(k[:, :, :], 1.0)) for k in KS]
        t_ks = t_ks[-1]

        loads = {}

        def load(b):
            for ring, st, key, name in ((xs, d_x, "x", "x"), (cs, d_cx, "c", "ctx_1024")):
                i = ring.at % len(st)
                s, free = ring.take()
                loads[key, b] = (s, sp.dma(st[i], s.ap[:, :], A[name][b], *free))

        def norm(x_ap, out, *toks):
            s, free = st6.take()
            a = dve.do(op_bn_stats, on(s.ap[:, 0:6], x_ap), *toks, *free)
            a = dve.do(op_bn_aggr, on(s.ap[:, 6:8], s.ap[:, 0:6]), a)
            a = dve.do(op_tensor_scalar, on(s.ap[:, 8:9], s.ap[:, 7:8], 1e-5, None, ALU.add), a)
            a = pool.do(op_tensor_tensor, on(s.ap[:, 9:10], s.ap[:, 8:9], nhalf[:, :], ALU.pow), a, t_nh)
            yield
            o, free = out
            a = dve.do(op_tensor_scalar, on(o, x_ap, s.ap[:, 6:7], s.ap[:, 9:10], ALU.subtract, ALU.mult),
                       a, *free)
            s.release(a)
            return a

        def transp(src, dst, toks, ring):
            p, pf = ring.take()
            a = pe.do(op_transpose, on(p.ap[:, 0:128], src, ident[:, :]), *toks, *pf)
            d, df = dst
            c = evac(d, p.ap[:, 0:128], a, *df)
            p.release(c)
            return a, c

        ST = {}

        def stage_a(b):
            x, tx = loads["x", b]
            ar, af = arow.take()
            ta = yield from norm(x.ap[:, :], (ar.ap[:, :], af), tx)
            xa, xf = xab.take()
            t1 = pool.do(op_tensor_tensor, on(xa.ap[:, :], x.ap[:, :], ar.ap[:, :], ALU.add), ta, *xf)
            t2 = pool.do(op_tensor_tensor, on(xa.ap[:, :], xa.ap[:, :], bo[:, :], ALU.add), t1, t_c)
            x.release(t1)
            at, atf = aT.take()
            tp, tc = transp(ar.ap[:, :], (at.ap[:, :], atf), [ta], rA)
            ar.release(tp, t1)
            yield
            p, pf = rA.take()
            pe.do(op_matmul, on(p.ap[:, 0:128], winT[:, 0:128], at.ap[:, :], start=True, stop=True),
                  tc, W["a"], *pf, sig=False)
            pe.do(op_matmul, on(p.ap[:, 128:256], winT[:, 128:256], at.ap[:, :], start=True, stop=True), sig=False)
            tm = pe.do(op_matmul, on(p.ap[:, 256:384], at.ap[:, :], winT[:, 256:384], start=True, stop=True))
            at.release(tm)
            q, qf = qk.take()
            tq = []
            for j in range(2):
                tq.append(act.do(op_activation, on(q.ap[:, j, :], p.ap[:, j * 128:j * 128 + 128],
                                                             ACT.Identity, bias=bqk[:, j:j + 1]), tm, t_c, *qf))
            vp, vf = vpad.take()
            tv = dve.do(op_tensor_tensor, on(vp.ap[:, :, 0:8],
                                                  p.ap[:, 256:384].rearrange("p (h d) -> p h d", h=NH),
                                                  bv[:, :].rearrange("p (h d) -> p h d", h=NH), ALU.add),
                        tm, t_c, tq[1], *t_vp, *vf)
            p.release(tq[1], tv)
            pt, ptf = parts.take()
            r, rf = res.take()
            yield
            a = act.do(op_activation, on(pt.ap[:, :, 0, :], q.ap[:, :, :], ACT.Copy), *tq, *ptf)
            a = pool.do(op_tensor_tensor, on(r.ap[:, :, :], q.ap[:, :, :], pt.ap[:, :, 0, :], ALU.subtract), a, *rf)
            q.release(a)
            yield
            a = act.do(op_activation, on(pt.ap[:, :, 1, :], r.ap[:, :, :], ACT.Copy), a)
            a = pool.do(op_tensor_tensor, on(pt.ap[:, :, 2, :], r.ap[:, :, :], pt.ap[:, :, 1, :], ALU.subtract), a)
            r.release(a)
            yield
            i = QS.at % 2
            Q, Qf = QS.take()
            K = KS[i]
            Z = A["z_qk"]
            ts = sp.dma(d_zs[b % 2], Z[b].rearrange("j m p t -> p j m t"), pt.ap[:, :, :, :], a)
            for g in range(3):
                for m in range(3):
                    sp.dma(d_sk[i], Q.ap[24 * g + 8 * m:24 * g + 8 * m + 8, :, :],
                           Z[b, 0, g].rearrange("(d h) t -> d h t", d=8), ts, *Qf)
                td = sp.dma(d_sk[i], K[24 * g:24 * g + 24, :, :],
                            Z[b, 1].rearrange("m (d h) t -> (m d) h t", d=8), ts, t_ks, *Qf)
            pt.release(ts)
            ST["A", b] = (xa, t2, vp, tv, Q, K, td)

        def stage_b1(b):
            xa, t2, vp, tv, Q, K, td = ST["A", b]
            m, mf = mxs.take()
            for g in range(4):
                p, pf = rS.take()
                for c in range(4):
                    h = 4 * g + c
                    t = pe.do(op_matmul, on(p.ap[:, c * 128:c * 128 + 128], Q.ap[0:72, h, :],
                                                           K[0:72, h, :], start=True, stop=True),
                              td, *pf, sig=(c == 3))
                    pf = []
                t = dve.do(op_tensor_reduce, on(m.ap[:, 4 * g:4 * g + 4],
                                                          p.ap.rearrange("p (h k) -> p h k", h=4), AX.X, ALU.max),
                           t, *mf)
                p.release(t)
                yield
            n, nf = nm.take()
            f = nmf[b % 2]
            a = dve.do(op_tensor_scalar, on(f[:, 0, :], m.ap[:, :], -1.0, None, ALU.mult), t, *nf)
            m.release(a)
            a = dve.do(op_tensor_copy, on(n.ap[:, 0, :], f[:, 0, :]), a)
            a = dve.do(op_tensor_tensor, on(f[:, 1, :], f[:, 0, :], n.ap[:, 0, :], ALU.subtract), a)
            a = dve.do(op_tensor_copy, on(n.ap[:, 1, :], f[:, 1, :]), a)
            a = dve.do(op_tensor_tensor, on(n.ap[:, 2, :], f[:, 1, :], n.ap[:, 1, :], ALU.subtract), a)
            yield
            p, pf = rA.take()
            pb = p.ap[0:48, 0:64].bitcast(BF16)
            a = pe.do(op_transpose, on(pb, n.ap[:, :, :].rearrange("p a h -> p (a h)"), identb[:, :]),
                      a, t_idb, *pf)
            c = act.do(op_activation, on(nmT[b % 2][:, :], pb, ACT.Copy), a, ST.get(("nmT", b % 2)))
            p.release(c)
            n.release(a)
            t = sp.dma(d_zn[b % 2], A["z_nm"][b], nmT[b % 2][:, :], c)
            tn = sp.dma(d_nm[b % 2], Q.ap[72:75, :, :], A["z_nm"][b].rearrange("(j h) t -> j h t", j=3), t)
            ST["nmT", b % 2] = t
            ST["B1", b] = tn

        def stage_b2(b):
            xa, t2, vp, tv, Q, K, td = ST["A", b]
            tn = ST["B1", b]
            o, of = rP.take()
            prev = None
            for g in range(5):
                if g < 4:
                    p, pf = rS.take()
                    for c in range(4):
                        h = 4 * g + c
                        t = pe.do(op_matmul, on(p.ap[:, c * 128:c * 128 + 128], K[0:75, h, :],
                                                               Q.ap[0:75, h, :], start=True, stop=True),
                                  tn, *pf, sig=(c == 3))
                        pf = []
                    if g == 3:
                        Q.release(t)
                    s, sf = PS.take()
                    te = act.do(op_activation, on(s.ap[:, :, :].rearrange("p h q -> p (h q)"), p.ap, ACT.Exp,
                                                       scale=S_SELF), t, *sf)
                    p.release(te)
                    now = (s, te)
                if prev:
                    s, te = prev
                    for c in range(4):
                        h = 4 * (g - 1) + c
                        tp = pe.do(op_matmul, on(
                            o.ap[32 * c:32 * c + 32, (g - 1) * 128:g * 128], vp.ap[:, h, :], s.ap[:, c, :],
                            start=True, stop=True), te, tv, *of, sig=(c == 3))
                        of = []
                    s.release(tp)
                prev = now
                yield
            vp.release(tp)
            ot, otf = oT.take()
            c = act.do(op_activation, on(ot.ap[:, :], o.ap, ACT.Copy), tp, *otf)
            o.release(c)
            p, pf = rA.take()
            for g in range(4):
                t = pe.do(op_transpose, on(p.ap[:, g * 128:g * 128 + 128], ot.ap[:, g * 128:g * 128 + 128],
                                                     ident[:, :]), c, *pf, sig=(g == 3))
                pf = []
            ot.release(t)
            pv = p.ap.rearrange("p (h d) -> p h d", h=NH)
            r, rf = rs.take()
            a = dve.do(op_reciprocal, on(r.ap[:, :].rearrange("p (h a) -> p h a", a=1), pv[:, :, 8:9]), t, *rf)
            n, nf = cn.take()
            a = dve.do(op_tensor_tensor, on(n.ap[:, :].rearrange("p (h d) -> p h d", h=NH), pv[:, :, 0:8],
                                                 r.ap[:, :].rearrange("p (h a) -> p h a", a=1).to_broadcast([128, NH, 8]),
                                                 ALU.mult), a, *nf)
            p.release(a)
            r.release(a)
            yield
            nt, ntf = cnT.take()
            tp, c = transp(n.ap[:, :], (nt.ap[:, :], ntf), [a], rA)
            n.release(tp)
            yield
            p, pf = rA.take()
            t = pe.do(op_matmul, on(p.ap[:, 0:128], nt.ap[:, :], woutT[:, :], start=True, stop=True), c, *pf)
            nt.release(t)
            x, xf = x1.take()
            a = dve.do(op_tensor_tensor, on(x.ap[:, :], p.ap[:, 0:128], xa.ap[:, :], ALU.add), t, t2, *xf)
            p.release(a)
            xa.release(a)
            yield
            l, lf = lnr.take()
            tl = yield from norm(x.ap[:, :], (l.ap[:, :], lf), a)
            ct, cf = cT.take()
            tp, c = transp(l.ap[:, :], (ct.ap[:, :], cf), [tl], rA)
            l.release(tp)
            ST["B", b] = (x, a, ct, c)

        def stage_c(b):
            cx, tcx = loads["c", b]
            xt, xf = cxT.take()
            tp, tk = transp(cx.ap[:, :], (xt.ap[:, :], xf), [tcx, t_c], rC)
            cx.release(tp)
            yield
            R, Rf = rot.take()
            x, a, ct, tq = ST["B", b]
            tr = []
            for j, src, ts, w, wj, name in ((1, xt, tk, wkT, wkJ, "L0_xattn_wk"), (0, ct, tq, wqT, wqJ, "L0_xattn_wq")):
                for half in range(2):
                    T, Tf = t12.take()
                    for m, (ww, tab) in enumerate(((w, cos), (wj, sin))):
                        p, pf = rC.take()
                        for c in range(4):
                            t = pe.do(op_matmul, on(p.ap[:, c * 128:c * 128 + 128], ww[:, 4 * half + c, :],
                                                              src.ap[:, :], start=True, stop=True),
                                      ts, W[name], *pf, sig=(c == 3))
                            pf = []
                        t = dve.do(op_tensor_tensor, on(
                            T.ap[:, m, :, :], p.ap.rearrange("p (c t) -> p c t", c=4),
                            tab[:, :].rearrange("p (a t) -> p a t", a=1).to_broadcast([128, 4, 128]), ALU.mult),
                            t, *Tf)
                        p.release(t)
                        yield
                    t = pool.do(op_tensor_tensor, on(R.ap[:, j, 4 * half:4 * half + 4, :], T.ap[:, 0, :, :],
                                                          T.ap[:, 1, :, :], ALU.add), t, *Rf)
                    T.release(t)
                    tr.append(t)
                if j == 0:
                    ct.release((pe.sem, pe.n))
            v, vf = V.take()
            tv = []
            for half in range(2):
                p, pf = rC.take()
                t = pe.do(op_matmul, on(p.ap, xt.ap[:, :],
                                             wvT[:, 4 * half:4 * half + 4, :].rearrange("p a n -> p (a n)"),
                                             start=True, stop=True), W["wv"], *pf)
                c = act.do(op_activation, on(v.ap[:, 8 * half:8 * half + 8, :].rearrange("p h d -> p (h d)"),
                                                  p.ap, ACT.Copy), t, *vf)
                p.release(c)
                tv.append(c)
                yield
            xt.release(t)
            ST["C", b] = (R, tr, v, tv)

        def stage_d(b):
            R, tr, v, tv = ST["C", b]
            x, tx1, _, _ = ST["B", b]
            m, mf = mx.take()
            nb, nbf = mx.take()
            sm, smf = mx.take()
            ri, rif = mx.take()
            hist = {}
            outs = []
            for g in range(7):
                if g < 4:
                    p, pf = rX.take()
                    pe.do(op_matmul, on(p.ap, identb[:, :], mask[:, :], start=True, stop=False,
                                             skip_group_check=True), t_idb, t_mask, *pf, sig=False)
                    for c in range(4):
                        q = 4 * (g // 2) + c
                        lo = 64 * (g % 2)
                        t = pe.do(op_matmul, on(
                            p.ap[:, c * 128:c * 128 + 128], R.ap[lo:lo + 64, 0, q, :],
                            R.ap[lo:lo + 64, 1, q, :], start=False, stop=(c == 3), skip_group_check=True),
                            tr, sig=(c == 3))
                    if g == 3:
                        R.release(t)
                    t = dve.do(op_tensor_reduce, on(m.ap[:, 4 * g:4 * g + 4],
                                                              p.ap.rearrange("p (h k) -> p h k", h=4), AX.X, ALU.max),
                               t, *mf)
                    t = dve.do(op_tensor_scalar, on(nb.ap[:, 4 * g:4 * g + 4], m.ap[:, 4 * g:4 * g + 4],
                                                              -S_X, None, ALU.mult), t, *nbf)
                    e_, ef = PX.take()
                    for c in range(4):
                        h = 4 * g + c
                        te = act.do(op_activation, on(
                            e_.ap[:, c, :], p.ap[:, c * 128:c * 128 + 128], ACT.Exp, bias=nb.ap[:, h:h + 1], scale=S_X,
                            accum_out=sm.ap[:, h:h + 1]), t, *ef, *smf)
                    p.release(te)
                    hist[g] = [e_, te]
                yield
                if 1 <= g < 5:
                    k = g - 1
                    e_, te = hist[k]
                    t = dve.do(op_reciprocal, on(ri.ap[:, 4 * k:4 * k + 4], sm.ap[:, 4 * k:4 * k + 4]), te, *rif)
                    n, nf = PN.take()
                    t = pool.do(op_tensor_tensor, on(
                        n.ap[:, :, :], e_.ap[:, :, :],
                        ri.ap[:, 4 * k:4 * k + 4].rearrange("p (h a) -> p h a", a=1).to_broadcast([128, 4, 128]),
                        ALU.mult), t, *nf)
                    e_.release(t)
                    hist[k] = [n, t]
                yield
                if 2 <= g < 6:
                    k = g - 2
                    n, tn = hist[k]
                    p, pf = rX.take()
                    for c in range(4):
                        t = pe.do(op_transpose, on(p.ap[:, c * 128:c * 128 + 128], n.ap[:, c, :],
                                                                  ident[:, :]), tn, *pf, sig=(c == 3))
                        pf = []
                    n.release(t)
                    pt, ptf = PT.take()
                    t = evac(pt.ap[:, :, :].rearrange("p h q -> p (h q)"), p.ap, t, *ptf)
                    p.release(t)
                    hist[k] = [pt, t]
                yield
                if 3 <= g:
                    k = g - 3
                    if k % 2:
                        o, of = rD.take()
                        for c in range(4):
                            for u in range(2):
                                pt, t = hist[k - 1 + u]
                                h = 4 * (k - 1) + 2 * c + u
                                tp = pe.do(op_matmul, on(
                                    o.ap[64 * u:64 * u + 64, c * 128:c * 128 + 128], v.ap[:, h, :], pt.ap[:, c, :],
                                    start=True, stop=True), t, tv, *of, sig=(c == 3 and u == 1))
                        hist[k][0].release(tp)
                        hist[k - 1][0].release(tp)
                        ox, oxf = oX.take()
                        t = evac(ox.ap[:, :, :].rearrange("p h q -> p (h q)"), o.ap, tp, *oxf)
                        o.release(t)
                        outs.append((ox, t))
            for s in (m, nb, sm, ri):
                s.release(te, tn)
            v.release(tp)
            yield
            p, pf = rD.take()
            for q in range(8):
                ox, to = outs[q // 4]
                t = pe.do(op_matmul, on(p.ap[:, 0:128], ox.ap[:, q % 4, :], woT[:, q, :],
                                                         start=(q == 0), stop=(q == 7)),
                          to, W["wo"], *pf, sig=(q == 7))
                pf = []
            for ox, _ in outs:
                ox.release(t)
            y, yf = x2.take()
            a = dve.do(op_tensor_tensor, on(y.ap[:, :], p.ap[:, 0:128], x.ap[:, :], ALU.add), t, tx1, *yf)
            p.release(a)
            x.release(a)
            yield
            l, lf = lnr.take()
            tl = yield from norm(y.ap[:, :], (l.ap[:, :], lf), a)
            et, ef = eT.take()
            tp, c = transp(l.ap[:, :], (et.ap[:, :], ef), [tl], rX)
            l.release(tp)
            ST["D", b] = (y, a, et, c)

        def stage_f(b):
            y, ty, et, te = ST["D", b]
            p, pf = rC.take()
            t = pe.do(op_matmul, on(p.ap[:, 0:8], et.ap[:, :], rtT[:, :], start=True, stop=True),
                      te, W["rt"], *pf)
            L, Lf = lg.take()
            U = lgu[b % 2]
            a = dve.do(op_tensor_copy, on(L.ap[:, 0:8], p.ap[:, 0:8]), t, *Lf)
            p.release(a)
            a = dve.do(op_max, on(L.ap[:, 8:16], L.ap[:, 0:8]), a)
            a = dve.do(op_max_index, on(U[:, :], L.ap[:, 8:16], L.ap[:, 0:8]), a)
            a = dve.do(op_tensor_copy, on(L.ap[:, 16:17], U[:, 0:1]), a)
            tw = dve.do(op_tensor_scalar, on(L.ap[:, 24:32], iota[:, :], L.ap[:, 16:17], 0.5,
                                                  ALU.is_equal, ALU.mult), a)
            yield
            hist = {}
            G, Gf = hT.take()
            ts = []
            for k in range(NE + 2):
                if k <= NE:
                    p, pf = rC.take()
                    t = pe.do(op_matmul, on(p.ap, et.ap[:, :], wgu[:, k, :], start=True, stop=True),
                              W["f"], *pf)
                    T, Tf = th.take()
                    t = act.do(op_activation, on(T.ap[:, 0, :], p.ap[:, 0:256], ACT.Tanh, scale=0.5), t, *Tf)
                    t = dve.do(op_scalar_tensor_tensor, on(out=T.ap[:, 1, :], in0=T.ap[:, 0, :], scalar=1.0,
                                                                in1=p.ap[:, 0:256], op0=ALU.add, op1=ALU.mult), t)
                    H, Hf = hb.take()
                    w = L.ap[:, 24 + k:25 + k] if k < NE else 0.5
                    t = dve.do(op_scalar_tensor_tensor, on(
                        out=H.ap[:, :, :].rearrange("p a n -> p (a n)"), in0=T.ap[:, 1, :], scalar=w,
                        in1=p.ap[:, 256:512], op0=ALU.mult, op1=ALU.mult), t, tw, *Hf)
                    p.release(t)
                    T.release(t)
                    hist[k] = (H, t)
                    if k == NE:
                        L.release(t)
                yield
                if 1 <= k <= NE + 1:
                    H, t = hist[k - 1]
                    p, pf = rC.take()
                    for c in range(2):
                        t = pe.do(op_transpose, on(p.ap[:, c * 128:c * 128 + 128], H.ap[:, c, :],
                                                                  ident[:, :]), t, *pf, sig=(c == 1))
                    H.release(t)
                    t = act.do(op_activation, on(G.ap[:, k - 1, :, :].rearrange("p a n -> p (a n)"),
                                                           p.ap[:, 0:256], ACT.Copy), t, *Gf)
                    p.release(t)
                    ts = [t]
                yield
            acc, af = rC.take()
            for k in range(NE + 1):
                for c in range(2):
                    t = pe.do(op_matmul, on(acc.ap[:, 0:128], G.ap[:, k, c, :], wd[:, k, c, :],
                                                           start=(k == 0 and c == 0), stop=(k == NE and c == 1)),
                              ts, *af, sig=(k == NE and c == 1))
            G.release(t)
            et.release(t)
            i = xo.at % 2
            o, of = xo.take()
            a = dve.do(op_tensor_tensor, on(o.ap[:, :], acc.ap[:, 0:128], y.ap[:, :], ALU.add), t, ty, *of)
            acc.release(a)
            y.release(a)
            o.release(sp.dma(d_o[i], A["out"][b], o.ap[:, :], a))

        rD = Ring(bank[0:0] + [bank[1]])
        rP = Ring([bank[3]])
        rA = Ring([bank[0]])
        rS = Ring([bank[2], bank[4]])
        rC = Ring([bank[5]])
        rX = Ring([bank[6], bank[7]])

        def weave(gens):
            gens = list(gens)
            while gens:
                for g in list(gens):
                    try:
                        next(g)
                    except StopIteration:
                        gens.remove(g)

        def run(g):
            for _ in g:
                pass

        LAG = {"A": 0, "B1": 1, "B2": 1, "C": 2, "D": 3, "F": 4}
        load(0)
        run(setup_a())

        def self_attn(b):
            yield from stage_b1(b)
            yield from stage_b2(b)

        for s in range(NB + 4):
            if s + 1 < NB:
                load(s + 1)
            gens = []
            if s == 0:
                gens.append(setup_f())
            if 0 <= s - 4 < NB:
                gens.append(stage_f(s - 4))
            if 0 <= s - 3 < NB:
                gens.append(stage_d(s - 3))
            if 0 <= s - 2 < NB:
                gens.append(stage_c(s - 2))
            if 0 <= s - 1 < NB:
                gens.append(self_attn(s - 1))
            if s < NB:
                gens.append(stage_a(s))
            weave(gens)
        for st in d_o:
            sp.wait((st[0], st[1]))

        block = ctx.enter_context(nc.Block())
        for name, q in (("sync", sp), ("tensor", pe), ("vector", dve), ("scalar", act), ("gpsimd", pool)):
            def body(eng, q=q):
                for op in q.ops:
                    op(eng)
            {"sync": block.sync, "tensor": block.tensor, "vector": block.vector, "scalar": block.scalar,
             "gpsimd": block.gpsimd}[name](body)


_INS = ['x', 'ctx_1024', 'L0_attn_w_in', 'L0_attn_b_in', 'L0_attn_w_out', 'L0_attn_b_out', 'L0_xattn_wq',
        'L0_xattn_wk', 'L0_xattn_wv', 'L0_xattn_wo', 'L0_ffn_up', 'L0_ffn_gate', 'L0_ffn_down', 'L0_ffn_router',
        'L0_ffn_w_up_s', 'L0_ffn_w_gate_s', 'L0_ffn_w_down_s']


def kernel(**inputs):
    import numpy as np
    import concourse.bacc as bacc
    from concourse.bass_utils import run_bass_kernel_spmd

    f = np.float32
    freqs = (f(1.0) / f(10000.0) ** (np.arange(0, 64, 2, dtype=f) / f(64))).astype(f)
    ang = np.arange(128, dtype=f)[:, None] * freqs[None, :]
    c, s = np.cos(ang).astype(f).T, np.sin(ang).astype(f).T
    i, j = np.arange(128)[:, None], np.arange(128)[None, :]
    band = np.where((j <= i) & (j >= i - 32), f(0), f(-1e30)).astype(f)
    arrays = {n: np.ascontiguousarray(inputs[n]) for n in _INS}
    arrays["ident"] = np.eye(128, dtype=f)
    arrays["cos"] = np.concatenate([c] * 4)
    arrays["sin"] = np.concatenate([-s, s, -s, s])
    arrays["mask"] = np.tile(band, (1, 4))
    arrays["iota"] = np.tile(np.arange(8, dtype=f), (128, 1))
    arrays["bqk"] = np.ascontiguousarray(
        arrays["L0_attn_b_in"][0:256].reshape(2, 16, 8).transpose(2, 1, 0).reshape(128, 2))
    arrays["bvb"] = np.ascontiguousarray(np.broadcast_to(arrays["L0_attn_b_in"][256:384], (128, 128)))
    arrays["bob"] = np.ascontiguousarray(np.broadcast_to(arrays["L0_attn_b_out"], (128, 128)))

    nc = bacc.Bacc("TRN2", target_bir_lowering=False, num_devices=1)
    A = {n: nc.dram_tensor(f"in_{n}", a.shape, mybir.dt.from_np(a.dtype), kind="ExternalInput").ap()
         for n, a in arrays.items()}
    A["out"] = nc.dram_tensor("out_0", (32, 128, 128), F32, kind="ExternalOutput").ap()
    A["z_qk"] = nc.dram_tensor("z_qk", (32, 2, 3, 128, 128), BF16, kind="Internal").ap()
    A["z_nm"] = nc.dram_tensor("z_nm", (32, 48, 128), BF16, kind="Internal").ap()
    build(nc, A)
    r = run_bass_kernel_spmd(nc, [{f"in_{n}": a for n, a in arrays.items()}], core_ids=[0])
    return r.results[0]["out_0"]
```

```python
from contextlib import ExitStack

import concourse.bass as bass
from concourse import mybir

F32 = mybir.dt.float32
BF16 = mybir.dt.bfloat16
U32 = mybir.dt.uint32
ALU = mybir.AluOpType
ACT = mybir.ActivationFunctionType
AX = mybir.AxisListType

NB = 32
NH = 16
NE = 8
S_SELF = float(8.0 ** -0.5)
S_X = 0.125
CHUNKS = [16, 16]
TILES = [n + 7 for n in CHUNKS]
NT = sum(TILES)


def on(*args, **kw):
    return args, kw


def op_activation(e, *x, **k):
    return e.activation(*x, **k)


def op_bn_aggr(e, *x, **k):
    return e.bn_aggr(*x, **k)


def op_bn_stats(e, *x, **k):
    return e.bn_stats(*x, **k)


def op_matmul(e, *x, **k):
    return e.matmul(*x, **k)


def op_max(e, *x, **k):
    return e.max(*x, **k)


def op_max_index(e, *x, **k):
    return e.max_index(*x, **k)


def op_memset(e, *x, **k):
    return e.memset(*x, **k)


def op_reciprocal(e, *x, **k):
    return e.reciprocal(*x, **k)


def op_scalar_tensor_tensor(e, *x, **k):
    return e.scalar_tensor_tensor(*x, **k)


def op_tensor_copy(e, *x, **k):
    return e.tensor_copy(*x, **k)


def op_tensor_reduce(e, *x, **k):
    return e.tensor_reduce(*x, **k)


def op_tensor_scalar(e, *x, **k):
    return e.tensor_scalar(*x, **k)


def op_tensor_tensor(e, *x, **k):
    return e.tensor_tensor(*x, **k)


def op_transpose(e, *x, **k):
    return e.transpose(*x, **k)


def op_matmul_expert(e, out, lhsT, table, n, index, start=True, stop=True):
    at = e.value_load(index, min_val=0, max_val=7 * n)
    return e.matmul(out, lhsT, table[:, bass.ds(at, n)], start=start, stop=stop)


def op_matmul_expert2(e, out, lhs, table, index):
    at = e.value_load(index, min_val=0, max_val=7 * 256)
    e.matmul(out, lhs[:, 0, :], table[:, bass.ds(at, 128)], start=True, stop=False)
    return e.matmul(out, lhs[:, 1, :], table[:, bass.ds(at + 128, 128)], start=False, stop=True)


def op_scatter(e, out, index, in_):
    return e.indirect_dma_start(out=out, out_offset=bass.IndirectOffsetOnAxis(ap=index, axis=0), in_=in_,
                                in_offset=None)


def op_gather(e, out, in_, index):
    return e.indirect_dma_start(out=out, out_offset=None, in_=in_,
                                in_offset=bass.IndirectOffsetOnAxis(ap=index, axis=0))


class Queue:

    def __init__(self, sem):
        self.sem, self.n, self.ops, self.seen = sem, 0, [], {}

    def wait(self, *toks):
        for t in toks:
            if t is None:
                continue
            if isinstance(t, list):
                self.wait(*t)
                continue
            sem, val = t
            if self.seen.get(id(sem), 0) < val:
                self.seen[id(sem)] = val
                self.ops.append(lambda e, sem=sem, val=val: e.wait_ge(sem, val))

    def do(self, fn, what, *toks, sig=True):
        self.wait(*toks)
        if not sig:
            self.ops.append(lambda e: fn(e, *what[0], **what[1]))
            return None
        self.n += 1
        self.ops.append(lambda e: fn(e, *what[0], **what[1]).then_inc(self.sem, 1))
        return (self.sem, self.n)

    def dma(self, stream, out, in_, *toks):
        self.wait(*toks)
        stream[1] += 16
        self.ops.append(lambda e: e.dma_start(out, in_).then_inc(stream[0], 16))
        return (stream[0], stream[1])

    def dma_by(self, fn, stream, what, *toks):
        self.wait(*toks)
        stream[1] += 16
        self.ops.append(lambda e: fn(e, *what[0]).then_inc(stream[0], 16))
        return (stream[0], stream[1])


class Slot:
    def __init__(self, ap):
        self.ap, self.free, self.held = ap, [], False

    def release(self, *toks):
        self.free = list(toks)
        self.held = False


class Ring:

    def __init__(self, aps):
        self.slots, self.at = [Slot(a) for a in aps], 0

    def take(self):
        s = self.slots[self.at % len(self.slots)]
        self.at += 1
        assert not s.held
        s.held = True
        return s, s.free


def build(nc, A):
    ctx = ExitStack()
    with ctx:
        def sb(name, shape, dt=F32):
            return ctx.enter_context(nc.sbuf_tensor(name, shape, dt))

        def sem(name):
            return ctx.enter_context(nc.semaphore(name))

        def stream(name):
            return [sem(name), 0]

        pe, dve, act, pool, sp = (Queue(sem(f"q_{n}")) for n in ("pe", "dve", "act", "pool", "sp"))

        P = ctx.enter_context(nc.psum_tensor("P", [128, 8, 512], F32))
        bank = [P[:, k, :] for k in range(8)]
        rA, rS, rC, rX = Ring(bank[0:2]), Ring(bank[2:4]), Ring(bank[4:6]), Ring(bank[6:8])

        ident = sb("ident", [128, 128])
        identb = sb("identb", [128, 128], BF16)
        cos = sb("cos", [128, 128])
        sin = sb("sin", [128, 128])
        mask = sb("mask", [128, 512], BF16)
        iota = sb("iota", [128, 8])
        zero = sb("zero", [128, 128])
        upper = sb("upper", [128, 128], BF16)
        ones = sb("ones", [128, 128], BF16)
        tri = sb("tri", [128, 8, 8])
        steps = sb("steps", [128, 32])
        OH = sb("OH", [128, NB, NE], BF16)
        pos = sb("pos", [128, NB], U32)
        exg = sb("exg", [128, NT], U32)
        exd = sb("exd", [128, NT], U32)
        nhalf = sb("nhalf", [128, 1])
        bqk = sb("bqk", [128, 2])
        bv = sb("bv", [128, 128])
        bo = sb("bo", [128, 128])
        winT = sb("winT", [128, 384])
        woutT = sb("woutT", [128, 128])
        wqT = sb("wqT", [128, 8, 128])
        wqJ = sb("wqJ", [128, 8, 128])
        wkT = sb("wkT", [128, 8, 128])
        wkJ = sb("wkJ", [128, 8, 128])
        wvT = sb("wvT", [128, 8, 128])
        woT = sb("woT", [128, 8, 128])
        rtT = sb("rtT", [128, 8])
        wgu = sb("wgu", [128, NE + 1, 512])
        wd = sb("wd", [128, NE + 1, 2, 128])
        xsum = sb("xsum", [128, NB, 128])
        stage = Ring([xsum[:, 8 * i:8 * i + 8, :] for i in range(4)])

        def staged(parts):
            s, free = stage.take()
            st = stage_stream[(stage.at - 1) % 4]
            for dst, src in parts:
                t = sp.dma(st, dst(s.ap), src, *free)
            return s, t

        stage_stream = [stream(f"d_st{i}") for i in range(4)]
        d_c = stream("d_c")
        for dst, src in ((ident, A["ident"]), (cos, A["cos"]), (sin, A["sin"]), (iota, A["iota"]),
                         (bqk, A["bqk"]), (bv, A["bvb"]),
                         (bo, A["bob"]), (steps, A["steps"]), (tri[:, :, :].rearrange("p a b -> p (a b)"), A["tri"])):
            t_c = sp.dma(d_c, dst[:, :], src)
        t_z = pool.do(op_memset, on(zero[:, :], 0.0))
        t_on = pool.do(op_memset, on(ones[:, :], 1.0))
        d_zero = stream("d_zero")
        t_idb = dve.do(op_tensor_copy, on(identb[:, :], ident[:, :]), t_c)
        t_nh = pool.do(op_memset, on(nhalf[:, :], -0.5))
        maskf, free = stage.take()
        st = stage_stream[(stage.at - 1) % 4]
        t = sp.dma(st, maskf.ap[:, 0:4, :], A["mask"].rearrange("p (a n) -> p a n", a=4))
        t_mask = dve.do(op_tensor_copy, on(mask[:, :].rearrange("p (a n) -> p a n", a=4), maskf.ap[:, 0:4, :]), t)
        maskf.release(t_mask)
        upf, free = stage.take()
        st = stage_stream[(stage.at - 1) % 4]
        t = sp.dma(st, upf.ap[:, 0, :], A["upper"])
        t_up = dve.do(op_tensor_copy, on(upper[:, :], upf.ap[:, 0, :]), t)
        upf.release(t_up)

        flip = [0]

        def evac(out, in_, *toks):
            flip[0] ^= 1
            if flip[0]:
                return dve.do(op_tensor_copy, on(out, in_), *toks)
            return act.do(op_activation, on(out, in_, ACT.Copy), *toks)

        def turn(s, t, n, outs, rows=128):
            done = []
            for b0 in range(0, n, 4):
                k = min(4, n - b0)
                p, pf = rA.take()
                for j in range(k):
                    tt = pe.do(op_transpose, on(p.ap[:, j * 128:j * 128 + rows],
                                                          s.ap[0:rows, b0 + j, :], ident[0:rows, 0:rows]),
                               t, t_c, *pf, sig=(j == k - 1))
                    pf = []
                ts = []
                for n_, (o, i) in enumerate(outs(b0, k, p.ap)):
                    if n_:
                        flip[0] ^= 1
                    ts.append(evac(o, i, tt))
                p.release(*ts)
                done += ts
                last = tt
            s.release(last)
            return done

        def v3(ap, k):
            return ap[:, 0:k * 128].rearrange("p (a n) -> p a n", a=k)

        W = {}

        def setup_a():
            s, t = staged([(lambda a: a[:, 0:3, :], A["L0_attn_w_in"].rearrange("(a p) d -> p a d", p=128)),
                           (lambda a: a[:, 3, :], A["L0_attn_w_out"])])
            W["a"] = turn(s, t, 4, lambda b0, k, p: [
                (winT[:, 0:256].rearrange("p (j d h) -> p j h d", j=2, d=8),
                 p[:, 0:256].rearrange("p (j h d) -> p j h d", j=2, d=8)),
                (winT[:, 256:384], p[:, 256:384]), (woutT[:, :], p[:, 384:512])])
            yield
            for name, dst, dj in (("L0_xattn_wk", wkT, wkJ), ("L0_xattn_wq", wqT, wqJ)):
                src = A[name].rearrange("(t h f e) d -> h e f t d", t=8, h=2, e=2)
                s, t = staged([(lambda a, q=2 * h + e: a[32 * q:32 * q + 32, :, :], src[h, e])
                               for h in range(2) for e in range(2)])

                def outs(b0, k, p, dst=dst, dj=dj):
                    pv = v3(p, 4)
                    o = [(dst[:, b0:b0 + 4, :], pv)]
                    for q in range(2):
                        o.append((dj[:, b0:b0 + 4, :].rearrange("p t (h e f) -> p t h e f", h=2, e=2)[:, :, :, q, :],
                                  pv.rearrange("p t (h e f) -> p t h e f", h=2, e=2)[:, :, :, 1 - q, :]))
                    return o
                W[name] = turn(s, t, 8, outs)
                yield
            s, t = staged([(lambda a: a[:, :, :], A["L0_xattn_wv"].rearrange("(t p) d -> p t d", p=128))])
            W["wv"] = turn(s, t, 8, lambda b0, k, p: [(wvT[:, b0:b0 + 4, :], v3(p, 4))])
            yield
            s, t = staged([(lambda a: a[:, :, :], A["L0_xattn_wo"].rearrange("o (t p) -> o t p", p=128))])
            W["wo"] = turn(s, t, 8, lambda b0, k, p: [(woT[:, b0:b0 + 4, :], v3(p, 4))])
            yield

        def setup_f():
            s, t = staged([(lambda a: a[0:8, 0, :], A["L0_ffn_router"])])
            W["rt"] = turn(s, t, 1, lambda b0, k, p: [(rtT[:, :], p[:, 0:8])], rows=8)
            yield
            W["f"] = []
            for half in range(2):
                for q, name in ((0, "L0_ffn_gate"), (1, "L0_ffn_up")):
                    src = A[name][4 * half:4 * half + 4].rearrange("e (t p) c -> p (e t) c", p=128)
                    s, t = staged([(lambda a: a[:, :, :], src)])
                    W["f"] += turn(s, t, 8, lambda b0, k, p, q=q, half=half: [
                        (wgu[:, 4 * half + b0 // 2:4 * half + b0 // 2 + 2, 256 * q:256 * q + 256],
                         p[:, :].rearrange("p (e n) -> p e n", e=2))])
                    yield
                src = A["L0_ffn_down"][4 * half:4 * half + 4].rearrange("e c (t h) -> c e t h", t=2)
                s, t = staged([(lambda a: a[:, :, :].rearrange("p (e t) h -> p e t h", t=2), src)])
                W["f"] += turn(s, t, 8, lambda b0, k, p, half=half: [
                    (wd[:, 4 * half + b0 // 2:4 * half + b0 // 2 + 2, :, :].rearrange("p e t n -> p (e t) n"), v3(p, 4))])
                yield
            s, t = staged([(lambda a: a[:, 0:2, :], A["L0_ffn_w_gate_s"].rearrange("(t p) c -> p t c", p=128)),
                           (lambda a: a[:, 2:4, :], A["L0_ffn_w_up_s"].rearrange("(t p) c -> p t c", p=128)),
                           (lambda a: a[:, 4:6, :], A["L0_ffn_w_down_s"].rearrange("c (t h) -> c t h", t=2))])

            def outs(b0, k, p):
                if b0 == 0:
                    return [(wgu[:, NE, :], p[:, :])]
                return [(wd[:, NE, :, :], v3(p, 2))]
            W["f"] += turn(s, t, 6, outs)
            yield

        xs = Ring([sb(f"x{i}", [128, 128]) for i in range(3)])
        d_x = [stream(f"d_x{i}") for i in range(3)]
        cs = Ring([sb(f"cx{i}", [128, 128]) for i in range(2)])
        d_cx = [stream(f"d_cx{i}") for i in range(2)]
        xab = Ring([sb(f"xab{i}", [128, 128]) for i in range(5)])
        arow = Ring([sb(f"arow{i}", [128, 128]) for i in range(2)])
        aT = Ring([sb(f"aT{i}", [128, 128]) for i in range(2)])
        qk = Ring([sb(f"qk{i}", [128, 2, 128]) for i in range(2)])
        res = Ring([sb(f"res{i}", [128, 2, 128]) for i in range(2)])
        parts = Ring([sb(f"parts{i}", [128, 2, 3, 128], BF16) for i in range(2)])
        d_sk = [stream(f"d_sk{i}") for i in range(3)]
        d_nm = [stream(f"d_nm{i}") for i in range(2)]
        d_zs = [stream(f"d_zs{i}") for i in range(2)]
        d_zn = [stream(f"d_zn{i}") for i in range(2)]
        vpad = Ring([sb(f"vpad{i}", [128, NH, 32]) for i in range(3)])
        QS = Ring([sb(f"QS{i}", [75, NH, 128], BF16) for i in range(3)])
        KS = [sb(f"KS{i}", [75, NH, 128], BF16) for i in range(3)]
        nm = Ring([sb(f"nm{i}", [128, 3, NH], BF16) for i in range(2)])
        nmf = [sb(f"nmf{i}", [128, 2, NH]) for i in range(2)]
        nmT = [sb(f"nmT{i}", [48, 128], BF16) for i in range(2)]
        PS = Ring([sb(f"PS{i}", [128, 4, 128]) for i in range(4)])
        oT = Ring([sb(f"oT{i}", [128, 512]) for i in range(2)])
        rs = Ring([sb(f"rs{i}", [128, NH]) for i in range(2)])
        cn = Ring([sb(f"cn{i}", [128, 128]) for i in range(2)])
        cnT = Ring([sb(f"cnT{i}", [128, 128]) for i in range(2)])
        x1 = Ring([sb(f"xi{i}", [128, 128]) for i in range(5)])
        lnr = Ring([sb(f"lnr{i}", [128, 128]) for i in range(3)])
        cT = Ring([sb(f"cT{i}", [128, 128]) for i in range(3)])
        cxT = Ring([sb(f"cxT{i}", [128, 128]) for i in range(2)])
        t12 = Ring([sb(f"t12_{i}", [128, 4, 128]) for i in range(2)])
        rot = Ring([sb(f"rot{i}", [128, 2, 8, 128]) for i in range(2)])
        V = Ring([sb(f"V{i}", [128, NH, 64]) for i in range(2)])
        mxs = Ring([sb(f"mxs{i}", [128, 16]) for i in range(2)])
        mx = Ring([sb(f"mx{i}", [128, 16]) for i in range(8)])
        PX = Ring([sb(f"PX{i}", [128, 4, 128]) for i in range(3)])
        PT = Ring([sb(f"PT{i}", [128, 4, 128]) for i in range(3)])
        oX = Ring([sb(f"oX{i}", [128, 4, 128]) for i in range(2)])
        erow = Ring([sb(f"er{i}", [128, 128]) for i in range(3)])
        d_er = [stream(f"d_er{i}") for i in range(3)]
        ers = Ring([sb(f"ers{i}", [128, 128]) for i in range(3)])
        d_ers = [stream(f"d_ers{i}") for i in range(3)]
        d_sc = [stream(f"d_sc{i}") for i in range(3)]
        xst = Ring([sb(f"xst{i}", [128, 128]) for i in range(3)])
        d_xst = [stream(f"d_xst{i}") for i in range(3)]
        yst = Ring([sb(f"yst{i}", [128, 128]) for i in range(3)])
        d_yst = [stream(f"d_yst{i}") for i in range(3)]
        yg = Ring([sb(f"yg{i}", [128, 128]) for i in range(3)])
        d_yg = [stream(f"d_yg{i}") for i in range(3)]
        xsT = Ring([sb(f"xsT{i}", [128, 128]) for i in range(2)])
        cnt = sb("cnt", [128, 96])
        cmpb = sb("cmpb", [128, 256])
        posf = sb("posf", [128, 160])
        exf = sb("exf", [128, 32])
        eT = Ring([sb(f"eT{i}", [128, 128]) for i in range(2)])
        st6 = Ring([sb(f"st6_{i}", [128, 12]) for i in range(6)])
        lg = Ring([sb(f"lg{i}", [128, 40]) for i in range(2)])
        lgu = [sb(f"lgu{i}", [128, 8], U32) for i in range(2)]
        th = Ring([sb(f"th{i}", [128, 2, 256]) for i in range(2)])
        hb = Ring([sb(f"hb{i}", [128, 2, 128]) for i in range(2)])
        hT = Ring([sb(f"hT{i}", [128, 2, 128]) for i in range(2)])
        xo = Ring([sb(f"xo{i}", [128, 128]) for i in range(2)])
        d_o = [stream(f"d_o{i}") for i in range(2)]

        t_vp = []
        for s in vpad.slots:
            a = dve.do(op_memset, on(s.ap[:, :, :], 0.0))
            t_vp.append(dve.do(op_memset, on(s.ap[:, :, 8:9], 1.0), a))
        t_ks = [dve.do(op_memset, on(k[:, :, :], 1.0)) for k in KS]
        t_ks = t_ks[-1]

        loads = {}

        def load(b, key, ring, st, name):
            i = ring.at % len(st)
            s, free = ring.take()
            loads[key, b] = (s, sp.dma(st[i], s.ap[:, :], A[name][b], *free))

        def norm(x_ap, out, *toks):
            s, free = st6.take()
            a = dve.do(op_bn_stats, on(s.ap[:, 0:6], x_ap), *toks, *free)
            a = dve.do(op_bn_aggr, on(s.ap[:, 6:8], s.ap[:, 0:6]), a)
            a = dve.do(op_tensor_scalar, on(s.ap[:, 8:9], s.ap[:, 7:8], 1e-5, None, ALU.add), a)
            a = pool.do(op_tensor_tensor, on(s.ap[:, 9:10], s.ap[:, 8:9], nhalf[:, :], ALU.pow), a, t_nh)
            yield
            o, free = out
            a = dve.do(op_tensor_scalar, on(o, x_ap, s.ap[:, 6:7], s.ap[:, 9:10], ALU.subtract, ALU.mult),
                       a, *free)
            s.release(a)
            return a

        def transp(src, dst, toks, ring):
            p, pf = ring.take()
            a = pe.do(op_transpose, on(p.ap[:, 0:128], src, ident[:, :]), *toks, *pf)
            d, df = dst
            c = evac(d, p.ap[:, 0:128], a, *df)
            p.release(c)
            return a, c

        ST = {}

        def stage_a(b):
            x, tx = loads["x", b]
            ar, af = arow.take()
            ta = yield from norm(x.ap[:, :], (ar.ap[:, :], af), tx)
            xa, xf = xab.take()
            t1 = pool.do(op_tensor_tensor, on(xa.ap[:, :], x.ap[:, :], ar.ap[:, :], ALU.add), ta, *xf)
            t2 = pool.do(op_tensor_tensor, on(xa.ap[:, :], xa.ap[:, :], bo[:, :], ALU.add), t1, t_c)
            x.release(t1)
            at, atf = aT.take()
            tp, tc = transp(ar.ap[:, :], (at.ap[:, :], atf), [ta], rA)
            ar.release(tp, t1)
            yield
            p, pf = rA.take()
            pe.do(op_matmul, on(p.ap[:, 0:128], winT[:, 0:128], at.ap[:, :], start=True, stop=True),
                  tc, W["a"], *pf, sig=False)
            pe.do(op_matmul, on(p.ap[:, 128:256], winT[:, 128:256], at.ap[:, :], start=True, stop=True), sig=False)
            tm = pe.do(op_matmul, on(p.ap[:, 256:384], at.ap[:, :], winT[:, 256:384], start=True, stop=True))
            at.release(tm)
            q, qf = qk.take()
            tq = []
            for j in range(2):
                tq.append(act.do(op_activation, on(q.ap[:, j, :], p.ap[:, j * 128:j * 128 + 128],
                                                             ACT.Identity, bias=bqk[:, j:j + 1]), tm, t_c, *qf))
            vp, vf = vpad.take()
            tv = dve.do(op_tensor_tensor, on(vp.ap[:, :, 0:8],
                                                  p.ap[:, 256:384].rearrange("p (h d) -> p h d", h=NH),
                                                  bv[:, :].rearrange("p (h d) -> p h d", h=NH), ALU.add),
                        tm, t_c, tq[1], *t_vp, *vf)
            p.release(tq[1], tv)
            pt, ptf = parts.take()
            r, rf = res.take()
            yield
            a = act.do(op_activation, on(pt.ap[:, :, 0, :], q.ap[:, :, :], ACT.Copy), *tq, *ptf)
            a = pool.do(op_tensor_tensor, on(r.ap[:, :, :], q.ap[:, :, :], pt.ap[:, :, 0, :], ALU.subtract), a, *rf)
            q.release(a)
            yield
            a = act.do(op_activation, on(pt.ap[:, :, 1, :], r.ap[:, :, :], ACT.Copy), a)
            a = pool.do(op_tensor_tensor, on(pt.ap[:, :, 2, :], r.ap[:, :, :], pt.ap[:, :, 1, :], ALU.subtract), a)
            r.release(a)
            yield
            i = QS.at % 3
            Q, Qf = QS.take()
            K = KS[i]
            Z = A["z_qk"]
            ts = sp.dma(d_zs[b % 2], Z[b].rearrange("j m p t -> p j m t"), pt.ap[:, :, :, :], a)
            for g in range(3):
                for m in range(3):
                    sp.dma(d_sk[i], Q.ap[24 * g + 8 * m:24 * g + 8 * m + 8, :, :],
                           Z[b, 0, g].rearrange("(d h) t -> d h t", d=8), ts, *Qf)
                td = sp.dma(d_sk[i], K[24 * g:24 * g + 24, :, :],
                            Z[b, 1].rearrange("m (d h) t -> (m d) h t", d=8), ts, t_ks, *Qf)
            pt.release(ts)
            ST["A", b] = (xa, t2, vp, tv, Q, K, td)

        def stage_b1(b):
            xa, t2, vp, tv, Q, K, td = ST["A", b]
            m, mf = mxs.take()
            for g in range(4):
                p, pf = rS.take()
                for c in range(4):
                    h = 4 * g + c
                    t = pe.do(op_matmul, on(p.ap[:, c * 128:c * 128 + 128], Q.ap[0:72, h, :],
                                                           K[0:72, h, :], start=True, stop=True),
                              td, *pf, sig=(c == 3))
                    pf = []
                t = dve.do(op_tensor_reduce, on(m.ap[:, 4 * g:4 * g + 4],
                                                          p.ap.rearrange("p (h k) -> p h k", h=4), AX.X, ALU.max),
                           t, *mf)
                p.release(t)
                yield
            n, nf = nm.take()
            f = nmf[b % 2]
            a = dve.do(op_tensor_scalar, on(f[:, 0, :], m.ap[:, :], -1.0, None, ALU.mult), t, *nf)
            m.release(a)
            a = dve.do(op_tensor_copy, on(n.ap[:, 0, :], f[:, 0, :]), a)
            a = dve.do(op_tensor_tensor, on(f[:, 1, :], f[:, 0, :], n.ap[:, 0, :], ALU.subtract), a)
            a = dve.do(op_tensor_copy, on(n.ap[:, 1, :], f[:, 1, :]), a)
            a = dve.do(op_tensor_tensor, on(n.ap[:, 2, :], f[:, 1, :], n.ap[:, 1, :], ALU.subtract), a)
            yield
            p, pf = rA.take()
            pb = p.ap[0:48, 0:64].bitcast(BF16)
            a = pe.do(op_transpose, on(pb, n.ap[:, :, :].rearrange("p a h -> p (a h)"), identb[:, :]),
                      a, t_idb, *pf)
            c = act.do(op_activation, on(nmT[b % 2][:, :], pb, ACT.Copy), a, ST.get(("nmT", b % 2)))
            p.release(c)
            n.release(a)
            t = sp.dma(d_zn[b % 2], A["z_nm"][b], nmT[b % 2][:, :], c)
            tn = sp.dma(d_nm[b % 2], Q.ap[72:75, :, :], A["z_nm"][b].rearrange("(j h) t -> j h t", j=3), t)
            ST["nmT", b % 2] = t
            ST["B1", b] = tn

        def stage_b2(b):
            xa, t2, vp, tv, Q, K, td = ST["A", b]
            tn = ST["B1", b]
            prev = []
            for g in range(4):
                p, pf = rS.take()
                for c in range(4):
                    h = 4 * g + c
                    t = pe.do(op_matmul, on(p.ap[:, c * 128:c * 128 + 128], K[0:75, h, :], Q.ap[0:75, h, :],
                                            start=True, stop=True), tn, *pf, sig=(c == 3))
                if g == 3:
                    Q.release(t)
                s, sf = PS.take()
                te = act.do(op_activation, on(s.ap[:, :, :].rearrange("p h q -> p (h q)"), p.ap, ACT.Exp,
                                              scale=S_SELF), t, *sf)
                p.release(te)
                prev.append((s, te))
                yield
            yield
            o, of = rA.take()
            for g in range(4):
                s, te = prev[g]
                for c in range(4):
                    h = 4 * g + c
                    tp = pe.do(op_matmul, on(o.ap[32 * c:32 * c + 32, g * 128:(g + 1) * 128], vp.ap[:, h, :],
                                             s.ap[:, c, :], start=True, stop=True), te, tv, *of, sig=(c == 3))
                s.release(tp)
            vp.release(tp)
            ot, otf = oT.take()
            c = act.do(op_activation, on(ot.ap[:, :], o.ap, ACT.Copy), tp, *otf)
            o.release(c)
            yield
            p, pf = rA.take()
            for g in range(4):
                t = pe.do(op_transpose, on(p.ap[:, g * 128:g * 128 + 128], ot.ap[:, g * 128:g * 128 + 128],
                                                     ident[:, :]), c, *pf, sig=(g == 3))
                pf = []
            ot.release(t)
            pv = p.ap.rearrange("p (h d) -> p h d", h=NH)
            r, rf = rs.take()
            a = dve.do(op_reciprocal, on(r.ap[:, :].rearrange("p (h a) -> p h a", a=1), pv[:, :, 8:9]), t, *rf)
            n, nf = cn.take()
            a = dve.do(op_tensor_tensor, on(n.ap[:, :].rearrange("p (h d) -> p h d", h=NH), pv[:, :, 0:8],
                                                 r.ap[:, :].rearrange("p (h a) -> p h a", a=1).to_broadcast([128, NH, 8]),
                                                 ALU.mult), a, *nf)
            p.release(a)
            r.release(a)
            yield
            nt, ntf = cnT.take()
            tp, c = transp(n.ap[:, :], (nt.ap[:, :], ntf), [a], rA)
            n.release(tp)
            yield
            p, pf = rA.take()
            t = pe.do(op_matmul, on(p.ap[:, 0:128], nt.ap[:, :], woutT[:, :], start=True, stop=True), c, *pf)
            nt.release(t)
            x, xf = x1.take()
            a = dve.do(op_tensor_tensor, on(x.ap[:, :], p.ap[:, 0:128], xa.ap[:, :], ALU.add), t, t2, *xf)
            p.release(a)
            xa.release(a)
            yield
            l, lf = lnr.take()
            tl = yield from norm(x.ap[:, :], (l.ap[:, :], lf), a)
            ct, cf = cT.take()
            tp, c = transp(l.ap[:, :], (ct.ap[:, :], cf), [tl], rA)
            l.release(tp)
            ST["B", b] = (x, a, ct, c)

        def stage_c(b):
            cx, tcx = loads["c", b]
            xt, xf = cxT.take()
            tp, tk = transp(cx.ap[:, :], (xt.ap[:, :], xf), [tcx, t_c], rC)
            cx.release(tp)
            yield
            R, Rf = rot.take()
            x, a, ct, tq = ST["B", b]
            tr = []
            for j, src, ts, w, wj, name in ((1, xt, tk, wkT, wkJ, "L0_xattn_wk"), (0, ct, tq, wqT, wqJ, "L0_xattn_wq")):
                for half in range(2):
                    T, Tf = t12.take()
                    for m, (ww, tab) in enumerate(((w, cos), (wj, sin))):
                        p, pf = rC.take()
                        for c in range(4):
                            t = pe.do(op_matmul, on(p.ap[:, c * 128:c * 128 + 128], ww[:, 4 * half + c, :],
                                                              src.ap[:, :], start=True, stop=True),
                                      ts, W[name], *pf, sig=(c == 3))
                            pf = []
                        t = dve.do(op_tensor_tensor, on(
                            T.ap[:, :, :] if m else R.ap[:, j, 4 * half:4 * half + 4, :],
                            p.ap.rearrange("p (c t) -> p c t", c=4),
                            tab[:, :].rearrange("p (a t) -> p a t", a=1).to_broadcast([128, 4, 128]), ALU.mult),
                            t, *Tf, *Rf)
                        p.release(t)
                        yield
                    t = pool.do(op_tensor_tensor, on(R.ap[:, j, 4 * half:4 * half + 4, :],
                                                   R.ap[:, j, 4 * half:4 * half + 4, :], T.ap[:, :, :], ALU.add), t)
                    T.release(t)
                    tr.append(t)
                if j == 0:
                    ct.release((pe.sem, pe.n))
            v, vf = V.take()
            tv = []
            for half in range(2):
                p, pf = rC.take()
                t = pe.do(op_matmul, on(p.ap, xt.ap[:, :],
                                             wvT[:, 4 * half:4 * half + 4, :].rearrange("p a n -> p (a n)"),
                                             start=True, stop=True), W["wv"], *pf)
                c = act.do(op_activation, on(v.ap[:, 8 * half:8 * half + 8, :].rearrange("p h d -> p (h d)"),
                                                  p.ap, ACT.Copy), t, *vf)
                p.release(c)
                tv.append(c)
                yield
            xt.release(t)
            ST["C", b] = (R, tr, v, tv)

        def stage_d(b):
            R, tr, v, tv = ST["C", b]
            x, tx1, _, _ = ST["B", b]
            m, mf = mx.take()
            nb, nbf = mx.take()
            sm, smf = mx.take()
            ri, rif = mx.take()
            hist = {}
            outs = []
            for g in range(7):
                if g < 4:
                    p, pf = rX.take()
                    pe.do(op_matmul, on(p.ap, identb[:, :], mask[:, :], start=True, stop=False,
                                             skip_group_check=True), t_idb, t_mask, *pf, sig=False)
                    for c in range(4):
                        q = 4 * (g // 2) + c
                        lo = 64 * (g % 2)
                        t = pe.do(op_matmul, on(
                            p.ap[:, c * 128:c * 128 + 128], R.ap[lo:lo + 64, 0, q, :],
                            R.ap[lo:lo + 64, 1, q, :], start=False, stop=(c == 3), skip_group_check=True),
                            tr, sig=(c == 3))
                    if g == 3:
                        R.release(t)
                    t = dve.do(op_tensor_reduce, on(m.ap[:, 4 * g:4 * g + 4],
                                                              p.ap.rearrange("p (h k) -> p h k", h=4), AX.X, ALU.max),
                               t, *mf)
                    t = dve.do(op_tensor_scalar, on(nb.ap[:, 4 * g:4 * g + 4], m.ap[:, 4 * g:4 * g + 4],
                                                              -S_X, None, ALU.mult), t, *nbf)
                    e_, ef = PX.take()
                    for c in range(4):
                        h = 4 * g + c
                        te = act.do(op_activation, on(
                            e_.ap[:, c, :], p.ap[:, c * 128:c * 128 + 128], ACT.Exp, bias=nb.ap[:, h:h + 1], scale=S_X,
                            accum_out=sm.ap[:, h:h + 1]), t, *ef, *smf)
                    p.release(te)
                    hist[g] = [e_, te]
                yield
                if 1 <= g < 5:
                    k = g - 1
                    e_, te = hist[k]
                    t = dve.do(op_reciprocal, on(ri.ap[:, 4 * k:4 * k + 4], sm.ap[:, 4 * k:4 * k + 4]), te, *rif)
                    n = e_
                    t = pool.do(op_tensor_tensor, on(
                        n.ap[:, :, :], n.ap[:, :, :],
                        ri.ap[:, 4 * k:4 * k + 4].rearrange("p (h a) -> p h a", a=1).to_broadcast([128, 4, 128]),
                        ALU.mult), t)
                    hist[k] = [n, t]
                yield
                if 2 <= g < 6:
                    k = g - 2
                    n, tn = hist[k]
                    p, pf = rX.take()
                    for c in range(4):
                        t = pe.do(op_transpose, on(p.ap[:, c * 128:c * 128 + 128], n.ap[:, c, :],
                                                                  ident[:, :]), tn, *pf, sig=(c == 3))
                        pf = []
                    n.release(t)
                    pt, ptf = PT.take()
                    t = evac(pt.ap[:, :, :].rearrange("p h q -> p (h q)"), p.ap, t, *ptf)
                    p.release(t)
                    hist[k] = [pt, t]
                yield
                if 3 <= g:
                    k = g - 3
                    if k % 2:
                        o, of = rA.take()
                        for c in range(4):
                            for u in range(2):
                                pt, t = hist[k - 1 + u]
                                h = 4 * (k - 1) + 2 * c + u
                                tp = pe.do(op_matmul, on(
                                    o.ap[64 * u:64 * u + 64, c * 128:c * 128 + 128], v.ap[:, h, :], pt.ap[:, c, :],
                                    start=True, stop=True), t, tv, *of, sig=(c == 3 and u == 1))
                        hist[k][0].release(tp)
                        hist[k - 1][0].release(tp)
                        ox, oxf = oX.take()
                        t = evac(ox.ap[:, :, :].rearrange("p h q -> p (h q)"), o.ap, tp, *oxf)
                        o.release(t)
                        outs.append((ox, t))
            for s in (m, nb, sm, ri):
                s.release(te, tn)
            v.release(tp)
            yield
            p, pf = rA.take()
            for q in range(8):
                ox, to = outs[q // 4]
                t = pe.do(op_matmul, on(p.ap[:, 0:128], ox.ap[:, q % 4, :], woT[:, q, :],
                                                         start=(q == 0), stop=(q == 7)),
                          to, W["wo"], *pf, sig=(q == 7))
                pf = []
            for ox, _ in outs:
                ox.release(t)
            y = xsum[:, b, :]
            a = dve.do(op_tensor_tensor, on(y, p.ap[:, 0:128], x.ap[:, :], ALU.add), t, tx1,
                       [q for s in stage.slots for q in s.free])
            p.release(a)
            x.release(a)
            yield
            i = erow.at % 3
            l, lf = erow.take()
            tl = yield from norm(y, (l.ap[:, :], lf), a)
            tz = sp.dma(d_er[i], A["z_e"][b], l.ap[:, :], tl)
            et, ef = eT.take()
            tp, c = transp(l.ap[:, :], (et.ap[:, :], ef), [tl], rX)
            l.release(tp, tz)
            ST["ze", b] = tz
            ST["D", b] = (y, a, et, c)

        def gated(p, T, Tf, H, Hf, t):
            t = act.do(op_activation, on(T.ap[:, 0, :], p.ap[:, 0:256], ACT.Tanh, scale=0.5), t, *Tf)
            t = dve.do(op_scalar_tensor_tensor, on(out=T.ap[:, 1, :], in0=T.ap[:, 0, :], scalar=1.0,
                                                   in1=p.ap[:, 0:256], op0=ALU.add, op1=ALU.mult), t)
            t = dve.do(op_scalar_tensor_tensor, on(out=H.ap[:, :, :].rearrange("p a n -> p (a n)"), in0=T.ap[:, 1, :],
                                                   scalar=0.5, in1=p.ap[:, 256:512], op0=ALU.mult, op1=ALU.mult),
                       t, *Hf)
            p.release(t)
            T.release(t)
            return t

        def stage_f(b):
            y, ty, et, te = ST["D", b]
            p, pf = rC.take()
            t = pe.do(op_matmul, on(p.ap[:, 0:8], et.ap[:, :], rtT[:, :], start=True, stop=True), te, W["rt"], *pf)
            L, Lf = lg.take()
            U = lgu[b % 2]
            a = dve.do(op_tensor_copy, on(L.ap[:, 0:8], p.ap[:, 0:8]), t, *Lf)
            p.release(a)
            a = dve.do(op_max, on(L.ap[:, 8:16], L.ap[:, 0:8]), a)
            a = dve.do(op_max_index, on(U[:, :], L.ap[:, 8:16], L.ap[:, 0:8]), a)
            a = dve.do(op_tensor_copy, on(L.ap[:, 16:17], U[:, 0:1]), a)
            a = dve.do(op_tensor_scalar, on(OH[:, b, :], iota[:, :], L.ap[:, 16:17], None, ALU.is_equal), a)
            L.release(a)
            ST["OH", b] = a
            yield
            p, pf = rC.take()
            for c in range(4):
                t = pe.do(op_matmul, on(p.ap[:, 128 * c:128 * c + 128], wgu[:, NE, 128 * c:128 * c + 128], et.ap[:, :],
                                        start=True, stop=True), te, W["f"], *pf, sig=(c == 3))
            et.release(t)
            T, Tf = th.take()
            H, Hf = hb.take()
            t = gated(p, T, Tf, H, Hf, t)
            yield
            p, pf = rC.take()
            for c in range(2):
                t = pe.do(op_matmul, on(p.ap[:, 0:128], H.ap[:, c, :], wd[:, NE, c, :], start=(c == 0), stop=(c == 1)),
                          t, *pf, sig=(c == 1))
            H.release(t)
            t = dve.do(op_tensor_tensor, on(y, p.ap[:, 0:128], y, ALU.add), t, ty)
            p.release(t)
            ST["F", b] = t

        wguf = wgu[:, 0:NE, :].rearrange("p e n -> p (e n)")
        wdf = wd[:, 0:NE, :, :].rearrange("p e t n -> p (e t n)")

        def dispatch(k):
            n, T = CHUNKS[k], TILES[k]
            b0, t0 = sum(CHUNKS[:k]), sum(TILES[:k])
            toh = [ST["OH", b0 + n - 1]]
            p, pf = rC.take()
            t = pe.do(op_matmul, on(p.ap[:, 0:8 * n], upper[:, :], OH[:, b0:b0 + n, :].rearrange("p b e -> p (b e)"),
                                    start=True, stop=False, skip_group_check=True), toh, t_up, t_on, *pf, sig=False)
            for i in range(n - 1):
                t = pe.do(op_matmul, on(p.ap[:, 8 * i + 8:8 * n].rearrange("p (b e) -> p b e", e=NE), ones[:, :],
                                        OH[:, b0 + i:b0 + i + 1, :].to_broadcast([128, n - 1 - i, NE]),
                                        start=False, stop=False, skip_group_check=True), sig=False)
            t = pe.do(op_matmul, on(p.ap[:, 0:8 * n], identb[:, :], zero[:, :].bitcast(BF16)[:, 0:8 * n],
                                    start=False, stop=True, skip_group_check=True), t_z)
            p2, p2f = rC.take()
            for i in range(n):
                t2 = pe.do(op_matmul, on(p2.ap[:, 0:8], ones[:, :], OH[:, b0 + i, :], start=(i == 0),
                                         stop=(i == n - 1)), *p2f, sig=(i == n - 1))
            free = ST.get("disp")
            a = dve.do(op_tensor_copy, on(cnt[:, 0:8], p2.ap[:, 0:8]), t2, free)
            p2.release(a)
            cm = cmpb[:, 0:8 * n].rearrange("p (e j) -> p e j", e=NE)
            a = dve.do(op_tensor_tensor, on(cm, cnt[:, 0:8].rearrange("p (e a) -> p e a", a=1).to_broadcast([128, NE, n]),
                                            steps[:, 0:n].rearrange("p (a j) -> p a j", a=1).to_broadcast([128, NE, n]),
                                            ALU.is_gt), a, t_c)
            a = dve.do(op_tensor_reduce, on(cnt[:, 8:16], cm, AX.X, ALU.add), a)
            c2 = cmpb[:, 0:64].rearrange("p (e f) -> p e f", e=NE)
            a = dve.do(op_tensor_tensor, on(c2, cnt[:, 8:16].rearrange("p (a f) -> p a f", a=1).to_broadcast([128, NE, NE]),
                                            tri[:, :, :], ALU.mult), a)
            a = dve.do(op_tensor_reduce, on(cnt[:, 16:24], c2, AX.X, ALU.add), a)
            a = dve.do(op_tensor_scalar, on(cnt[:, 24:32], cnt[:, 16:24], 128.0, None, ALU.mult), a)
            a = dve.do(op_tensor_tensor, on(cnt[:, 32:40], cnt[:, 16:24], cnt[:, 8:16], ALU.add), a)
            a = dve.do(op_tensor_scalar, on(cnt[:, 40:48], cnt[:, 32:40], 128.0, None, ALU.mult), a)
            pv = posf[:, 0:8 * n].rearrange("p (b e) -> p b e", e=NE)
            d = dve.do(op_tensor_tensor, on(pv, p.ap[:, 0:8 * n].rearrange("p (b e) -> p b e", e=NE),
                                            cnt[:, 24:32].rearrange("p (a e) -> p a e", a=1).to_broadcast([128, n, NE]),
                                            ALU.add), a, t)
            p.release(d)
            d = dve.do(op_tensor_tensor, on(pv, pv, OH[:, b0:b0 + n, :], ALU.mult), d)
            d = dve.do(op_tensor_reduce, on(posf[:, 128:128 + n], pv, AX.X, ALU.add), d)
            d = dve.do(op_tensor_copy, on(pos[:, b0:b0 + n], posf[:, 128:128 + n]), d)
            yield
            c3 = cmpb[:, 0:8 * T].rearrange("p (j e) -> p j e", e=NE)
            a = dve.do(op_tensor_tensor, on(c3, cnt[:, 40:48].rearrange("p (a e) -> p a e", a=1).to_broadcast([128, T, NE]),
                                            steps[:, 0:T].rearrange("p (j a) -> p j a", a=1).to_broadcast([128, T, NE]),
                                            ALU.is_le), a, d)
            a = dve.do(op_tensor_reduce, on(exf[:, 0:T], c3, AX.X, ALU.add), a)
            a = dve.do(op_tensor_scalar, on(exf[:, 0:T], exf[:, 0:T], 7.0, None, ALU.min), a)
            a1 = dve.do(op_tensor_scalar, on(exg[:, t0:t0 + T], exf[:, 0:T], 512.0, None, ALU.mult), a)
            a2 = dve.do(op_tensor_scalar, on(exd[:, t0:t0 + T], exf[:, 0:T], 256.0, None, ALU.mult), a)
            ST["disp"] = a2
            ST["ex", k] = [a1, a2]
            ts = []
            for b in range(b0, b0 + n):
                i = ers.at % 3
                r, rf = ers.take()
                tr = sp.dma(d_ers[i], r.ap[:, :], A["z_e"][b], ST["ze", b], *rf)
                t = pool.dma_by(op_scatter, d_sc[i], on(A["z_xs"][k], pos[:, b:b + 1], r.ap[:, :]), tr, d, t_zero)
                r.release(t)
                ts.append(t)
                if b % 4 == 3:
                    yield
            ST["xs", k] = ts[-3:]
            ST["pos", k] = d

        def tile(k, j):
            r0 = 128 * (j - sum(TILES[:k]))
            i = xst.at % 3
            x, xf = xst.take()
            t = sp.dma(d_xst[i], x.ap[:, :], A["z_xs"][k][r0:r0 + 128, :], ST["xs", k], *xf)
            yield
            xt, xtf = xsT.take()
            tp, t = transp(x.ap[:, :], (xt.ap[:, :], xtf), [t], rC)
            x.release(tp)
            yield
            p, pf = rC.take()
            t = pe.do(op_matmul_expert, on(p.ap, xt.ap[:, :], wguf, 512, exg[0:1, j:j + 1]), t, ST["ex", k], *pf)
            xt.release(t)
            T, Tf = th.take()
            H, Hf = hb.take()
            t = gated(p, T, Tf, H, Hf, t)
            yield
            p, pf = rC.take()
            for c in range(2):
                t = pe.do(op_transpose, on(p.ap[:, c * 128:c * 128 + 128], H.ap[:, c, :], ident[:, :]), t, *pf,
                          sig=(c == 1))
            H.release(t)
            G, Gf = hT.take()
            t = evac(G.ap[:, :, :].rearrange("p a n -> p (a n)"), p.ap[:, 0:256], t, *Gf)
            p.release(t)
            yield
            p, pf = rC.take()
            t = pe.do(op_matmul_expert2, on(p.ap[:, 0:128], G.ap, wdf, exd[0:1, j:j + 1]), t, *pf)
            G.release(t)
            i = yst.at % 3
            y, yf = yst.take()
            t = evac(y.ap[:, :], p.ap[:, 0:128], t, *yf)
            p.release(t)
            t = sp.dma(d_yst[i], A["z_ys"][k][r0:r0 + 128, :], y.ap[:, :], t)
            y.release(t)
            ST.setdefault(("ys", k), []).append(t)

        def collect(k):
            n = CHUNKS[k]
            b0 = sum(CHUNKS[:k])
            for b in range(b0, b0 + n):
                i = yg.at % 3
                y, yf = yg.take()
                t = pool.dma_by(op_gather, d_yg[i], on(y.ap[:, :], A["z_ys"][k], pos[:, b:b + 1]), ST["pos", k],
                                ST["ys", k][-3:], *yf)
                i = xo.at % 2
                o, of = xo.take()
                a = dve.do(op_tensor_tensor, on(o.ap[:, :], y.ap[:, :], xsum[:, b, :], ALU.add), t, ST["F", b], *of)
                y.release(a)
                o.release(sp.dma(d_o[i], A["out"][b], o.ap[:, :], a))
                yield

        rA, rS, rC, rX = Ring(bank[0:2]), Ring(bank[2:4]), Ring(bank[4:6]), Ring(bank[6:8])

        length = {}

        def counted(kind, g):
            n = 0
            for _ in g:
                n += 1
                yield
            length[kind] = n + 1

        def weave(gens):
            live = []
            for r, (kind, g) in enumerate(gens):
                live.append([0.0, r, 1.0 / length.get(kind, 12), counted(kind, g)])
            while live:
                live.sort(key=lambda v: (v[0], v[1]))
                v = live[0]
                try:
                    next(v[3])
                    v[0] += v[2]
                except StopIteration:
                    live.pop(0)

        def run(g):
            for _ in g:
                pass

        for k, n in enumerate(TILES):
            for j in range(n):
                t_zero = sp.dma(d_zero, A["z_xs"][k][j * 128:(j + 1) * 128, :], zero[:, 0:128], t_z)
        load(0, "x", xs, d_x, "x")
        run(setup_a())

        def chain(gens):
            for g in gens:
                yield from g

        order = (("F", stage_f, 5), ("D", stage_d, 4), ("C", stage_c, 3), ("B2", stage_b2, 2), ("B1", stage_b1, 1),
                 ("A", stage_a, 0))
        todo = []
        for s in range(NB + 5):
            if s + 1 < NB:
                load(s + 1, "x", xs, d_x, "x")
            if 0 <= s - 2 < NB:
                load(s - 2, "c", cs, d_cx, "ctx_1024")
            gens = []
            if s == 0:
                gens.append(("setup", setup_f()))
            for kind, f, lag in order:
                if 0 <= s - lag < NB:
                    gens.append((kind, f(s - lag)))
            if todo:
                gens.append(todo.pop(0))
            weave(gens)
            done = s - 5 + 1
            for k in range(len(CHUNKS)):
                if done == sum(CHUNKS[:k + 1]):
                    t0 = sum(TILES[:k])
                    todo.append(("dispatch", dispatch(k)))
                    if k < len(CHUNKS) - 1:
                        for j in range(0, TILES[k], 2):
                            todo.append((f"tile{min(2, TILES[k] - j)}",
                                         chain([tile(k, t0 + j + u) for u in range(min(2, TILES[k] - j))])))
                        todo.append(("collect", collect(k)))
        while todo:
            run(todo.pop(0)[1])
        k = len(CHUNKS) - 1
        waiting = [tile(k, sum(TILES[:k]) + j) for j in range(TILES[k])]
        live = []
        while waiting or live:
            if waiting:
                live.append(waiting.pop(0))
            for g in list(live):
                try:
                    next(g)
                except StopIteration:
                    live.remove(g)
        run(collect(k))
        for st in d_o:
            sp.wait((st[0], st[1]))

        block = ctx.enter_context(nc.Block())
        for name, q in (("sync", sp), ("tensor", pe), ("vector", dve), ("scalar", act), ("gpsimd", pool)):
            def body(eng, q=q):
                for op in q.ops:
                    op(eng)
            {"sync": block.sync, "tensor": block.tensor, "vector": block.vector, "scalar": block.scalar,
             "gpsimd": block.gpsimd}[name](body)


_INS = ['x', 'ctx_1024', 'L0_attn_w_in', 'L0_attn_b_in', 'L0_attn_w_out', 'L0_attn_b_out', 'L0_xattn_wq',
        'L0_xattn_wk', 'L0_xattn_wv', 'L0_xattn_wo', 'L0_ffn_up', 'L0_ffn_gate', 'L0_ffn_down', 'L0_ffn_router',
        'L0_ffn_w_up_s', 'L0_ffn_w_gate_s', 'L0_ffn_w_down_s']


def kernel(**inputs):
    import numpy as np
    import concourse.bacc as bacc
    from concourse.bass_utils import run_bass_kernel_spmd

    f = np.float32
    freqs = (f(1.0) / f(10000.0) ** (np.arange(0, 64, 2, dtype=f) / f(64))).astype(f)
    ang = np.arange(128, dtype=f)[:, None] * freqs[None, :]
    c, s = np.cos(ang).astype(f).T, np.sin(ang).astype(f).T
    i, j = np.arange(128)[:, None], np.arange(128)[None, :]
    band = np.where((j <= i) & (j >= i - 32), f(0), f(-1e30)).astype(f)
    arrays = {n: np.ascontiguousarray(inputs[n]) for n in _INS}
    arrays["ident"] = np.eye(128, dtype=f)
    arrays["cos"] = np.concatenate([c] * 4)
    arrays["sin"] = np.concatenate([-s, s, -s, s])
    arrays["mask"] = np.tile(band, (1, 4))
    arrays["iota"] = np.tile(np.arange(8, dtype=f), (128, 1))
    arrays["steps"] = np.tile(np.arange(32, dtype=f) * f(128), (128, 1))
    arrays["tri"] = np.tile(np.tril(np.ones((8, 8), f), -1).reshape(1, 64), (128, 1))
    arrays["upper"] = np.triu(np.ones((128, 128), f), 1)
    arrays["bqk"] = np.ascontiguousarray(
        arrays["L0_attn_b_in"][0:256].reshape(2, 16, 8).transpose(2, 1, 0).reshape(128, 2))
    arrays["bvb"] = np.ascontiguousarray(np.broadcast_to(arrays["L0_attn_b_in"][256:384], (128, 128)))
    arrays["bob"] = np.ascontiguousarray(np.broadcast_to(arrays["L0_attn_b_out"], (128, 128)))

    nc = bacc.Bacc("TRN2", target_bir_lowering=False, num_devices=1)
    A = {n: nc.dram_tensor(f"in_{n}", a.shape, mybir.dt.from_np(a.dtype), kind="ExternalInput").ap()
         for n, a in arrays.items()}
    A["out"] = nc.dram_tensor("out_0", (32, 128, 128), F32, kind="ExternalOutput").ap()
    A["z_qk"] = nc.dram_tensor("z_qk", (32, 2, 3, 128, 128), BF16, kind="Internal").ap()
    A["z_nm"] = nc.dram_tensor("z_nm", (32, 48, 128), BF16, kind="Internal").ap()
    A["z_e"] = nc.dram_tensor("z_e", (32, 128, 128), F32, kind="Internal").ap()
    A["z_xs"] = [nc.dram_tensor(f"z_xs{i}", (n * 128, 128), F32, kind="Internal").ap() for i, n in enumerate(TILES)]
    A["z_ys"] = [nc.dram_tensor(f"z_ys{i}", (n * 128, 128), F32, kind="Internal").ap() for i, n in enumerate(TILES)]
    build(nc, A)
    r = run_bass_kernel_spmd(nc, [{f"in_{n}": a for n, a in arrays.items()}], core_ids=[0])
    return r.results[0]["out_0"]
```

```python
from contextlib import ExitStack

import concourse.bass as bass
from concourse import mybir

F32 = mybir.dt.float32
BF16 = mybir.dt.bfloat16
U32 = mybir.dt.uint32
ALU = mybir.AluOpType
ACT = mybir.ActivationFunctionType
AX = mybir.AxisListType

NB = 32
NH = 16
NE = 8
S_SELF = float(8.0 ** -0.5)
S_X = 0.125
CHUNKS = [20, 12]
SETUP = [0, 0]
DEPTH = 6
LEAD = {"A": -0.7, "B1": -2.65, "B2": 3.15, "C": 2.4, "R": [-1.75, -0.2, -1.2, -0.8], "D": -4.6, "E": -0.25, "F": 0.75, "tile": 0.45, "rate": 0.425}
TILES = [n + 7 for n in CHUNKS]
NT = sum(TILES)


def on(*args, **kw):
    return args, kw


def op_activation(e, *x, **k):
    return e.activation(*x, **k)


def op_bn_aggr(e, *x, **k):
    return e.bn_aggr(*x, **k)


def op_bn_stats(e, *x, **k):
    return e.bn_stats(*x, **k)


def op_matmul(e, *x, **k):
    return e.matmul(*x, **k)


def op_max(e, *x, **k):
    return e.max(*x, **k)


def op_max_index(e, *x, **k):
    return e.max_index(*x, **k)


def op_memset(e, *x, **k):
    return e.memset(*x, **k)


def op_reciprocal(e, *x, **k):
    return e.reciprocal(*x, **k)


def op_scalar_tensor_tensor(e, *x, **k):
    return e.scalar_tensor_tensor(*x, **k)


def op_tensor_copy(e, *x, **k):
    return e.tensor_copy(*x, **k)


def op_tensor_reduce(e, *x, **k):
    return e.tensor_reduce(*x, **k)


def op_tensor_scalar(e, *x, **k):
    return e.tensor_scalar(*x, **k)


def op_tensor_tensor(e, *x, **k):
    return e.tensor_tensor(*x, **k)


def op_transpose(e, *x, **k):
    return e.transpose(*x, **k)


def op_load_expert(e, at, index_g, index_d):
    at.append(e.value_load(index_g, min_val=0, max_val=7 * 512))
    at.append(e.value_load(index_d, min_val=0, max_val=7 * 256))


def op_matmul_expert(e, out, lhsT, table, at):
    return e.matmul(out, lhsT, table[:, bass.ds(at[0], 512)], start=True, stop=True)


def op_matmul_expert2(e, out, lhs, table, at):
    e.matmul(out, lhs[:, 0, :], table[:, bass.ds(at[1], 128)], start=True, stop=False)
    return e.matmul(out, lhs[:, 1, :], table[:, bass.ds(at[1] + 128, 128)], start=False, stop=True)


def op_dma_start(e, *x):
    return e.dma_start(*x)


def op_scatter(e, out, index, in_):
    return e.indirect_dma_start(out=out, out_offset=bass.IndirectOffsetOnAxis(ap=index, axis=0), in_=in_,
                                in_offset=None)


def op_gather(e, out, in_, index):
    return e.indirect_dma_start(out=out, out_offset=None, in_=in_,
                                in_offset=bass.IndirectOffsetOnAxis(ap=index, axis=0))


def size(ap):
    n = 1
    for k in ap.shape[1:]:
        n *= k
    return n


def pe_ns(fn, x, k):
    if fn is op_load_expert:
        return 200
    if fn is op_matmul_expert:
        return 900
    if fn is op_matmul_expert2:
        return 480
    out, w = x[0], x[1]
    n = max(size(out), 64)
    if fn is op_transpose:
        return n * (0.84 if w.dtype == F32 else 0.42)
    ns = n / 2.4 * (4 if w.dtype == F32 else 1)
    return ns * {32: 0.35, 64: 0.63}.get(out.shape[0], 1)


def dve_ns(fn, x, k):
    n = max(size(a) for a in (*x[0:2], k.get("out"), k.get("in0")) if hasattr(a, "shape"))
    return (105 if fn is op_reciprocal else 65) + 1.05 * n


def act_ns(fn, x, k):
    return 53 + 0.83 * size(x[0]) + (93 if "accum_out" in k else 0) + (93 if "bias" in k else 0)


def pool_ns(fn, x, k):
    if fn is op_memset:
        return 40 + size(x[0]) * 0.8
    return 210 + (1.98 if size(x[0]) < 512 or x[-1] is ALU.add else 1.55) * size(x[0])


DMA_NS = 2400


def when(toks):
    t = 0
    for k in toks:
        if isinstance(k, Ring):
            s = k.next()
            t = max(t, when(s.free) if s else 1e9)
        elif isinstance(k, (list, set)) or (isinstance(k, tuple) and (not k or isinstance(k[0], tuple))):
            t = max(t, when(k))
        elif k:
            t = max(t, k[2])
    return t


class Queue:

    def __init__(self, sem, cost, lag):
        self.sem, self.n, self.ops, self.seen, self.cost, self.lag, self.clock = sem, 0, [], {}, cost, lag, 0

    def wait(self, *toks):
        for t in toks:
            if t is None:
                continue
            if isinstance(t, list):
                self.wait(*t)
                continue
            sem, val, _ = t
            if self.seen.get(id(sem), 0) < val:
                self.seen[id(sem)] = val
                self.ops.append(lambda e, sem=sem, val=val: e.wait_ge(sem, val))

    def do(self, fn, what, *toks, sig=True):
        self.wait(*toks)
        self.clock = max(self.clock, when(toks)) + self.cost(fn, *what)
        if not sig:
            self.ops.append(lambda e: fn(e, *what[0], **what[1]))
            return None
        self.n += 1
        self.ops.append(lambda e: fn(e, *what[0], **what[1]).then_inc(self.sem, 1))
        return (self.sem, self.n, self.clock + self.lag)

    def dma(self, stream, out, in_, *toks):
        return self.dma_by(op_dma_start, stream, on(out, in_), *toks)

    def dma_by(self, fn, stream, what, *toks):
        self.wait(*toks)
        stream[1] += 16
        self.clock = max(self.clock, when(toks)) + (450 if fn is op_dma_start else 1000)
        self.ops.append(lambda e: fn(e, *what[0]).then_inc(stream[0], 16))
        return (stream[0], stream[1], self.clock + DMA_NS)


class Slot:
    def __init__(self, ap, i):
        self.ap, self.i, self.free, self.held = ap, i, [], False

    def release(self, *toks):
        self.free = list(toks)
        self.held = False


class Ring:

    def __init__(self, aps):
        self.slots, self.at = [Slot(a, i) for i, a in enumerate(aps)], 0

    def next(self):
        n = len(self.slots)
        for i in range(n):
            s = self.slots[(self.at + i) % n]
            if not s.held:
                return s
        return None

    def take(self):
        s = self.next()
        assert s, f"all buffers are held: {self.slots[0].ap}"
        self.at = (s.i + 1) % len(self.slots)
        s.held = True
        return s, s.free


class Banks(Ring):

    def next(self):
        return min((s for s in self.slots if not s.held), key=lambda s: when(s.free), default=None)


def build(nc, A):
    ctx = ExitStack()
    with ctx:
        def sb(name, shape, dt=F32):
            return ctx.enter_context(nc.sbuf_tensor(name, shape, dt))

        def sem(name):
            return ctx.enter_context(nc.semaphore(name))

        def stream(name):
            return [sem(name), 0]

        pe, dve, act, pool, sp = (Queue(sem(f"q_{n}"), cost, lag) for n, cost, lag in (
            ("pe", pe_ns, 200), ("dve", dve_ns, 140), ("act", act_ns, 180), ("pool", pool_ns, 90), ("sp", None, 0)))

        P = ctx.enter_context(nc.psum_tensor("P", [128, 8, 512], F32))
        bank = [P[:, k, :] for k in range(8)]
        ps = Banks(bank)

        ident = sb("ident", [128, 128])
        identb = sb("identb", [128, 128], BF16)
        cos = sb("cos", [128, 128])
        sin = sb("sin", [128, 128])
        mask = sb("mask", [128, 128], BF16)
        iota = sb("iota", [128, 8])
        zero = sb("zero", [128, 128])
        upper = sb("upper", [128, 128], BF16)
        ones = sb("ones", [128, 128], BF16)
        tri = sb("tri", [128, 8, 8])
        steps = sb("steps", [128, 32])
        OH = sb("OH", [128, NB, NE], BF16)
        pos = sb("pos", [128, NB], U32)
        exg = sb("exg", [128, NT], U32)
        exd = sb("exd", [128, NT], U32)
        nhalf = sb("nhalf", [128, 1])
        bqk = sb("bqk", [128, 2])
        bv = sb("bv", [128, 128])
        bo = sb("bo", [128, 128])
        winT = sb("winT", [128, 384])
        woutT = sb("woutT", [128, 128])
        wqT = sb("wqT", [128, 8, 128])
        wqJ = sb("wqJ", [128, 8, 128])
        wkT = sb("wkT", [128, 8, 128])
        wkJ = sb("wkJ", [128, 8, 128])
        wvT = sb("wvT", [128, 8, 128])
        woT = sb("woT", [128, 8, 128])
        rtT = sb("rtT", [128, 8])
        wgu = sb("wgu", [128, NE + 1, 512])
        wd = sb("wd", [128, NE + 1, 2, 128])
        xsum = sb("xsum", [128, NB, 128])
        stage = Ring([xsum[:, 8 * i:8 * i + 8, :] for i in range(4)])

        def staged(parts):
            s, free = stage.take()
            st = stage_stream[(stage.at - 1) % 4]
            for dst, src in parts:
                t = sp.dma(st, dst(s.ap), src, *free)
            return s, t

        stage_stream = [stream(f"d_st{i}") for i in range(4)]
        d_c = stream("d_c")
        for dst, src in ((ident, A["ident"]), (cos, A["cos"]), (sin, A["sin"]), (iota, A["iota"]),
                         (bqk, A["bqk"]), (bv, A["bvb"]),
                         (bo, A["bob"]), (steps, A["steps"]), (tri[:, :, :].rearrange("p a b -> p (a b)"), A["tri"])):
            t_c = sp.dma(d_c, dst[:, :], src)
        t_z = pool.do(op_memset, on(zero[:, :], 0.0))
        t_on = pool.do(op_memset, on(ones[:, :], 1.0))
        d_zero = stream("d_zero")
        t_idb = dve.do(op_tensor_copy, on(identb[:, :], ident[:, :]), t_c)
        t_nh = pool.do(op_memset, on(nhalf[:, :], -0.5))
        maskf, free = stage.take()
        st = stage_stream[(stage.at - 1) % 4]
        t = sp.dma(st, maskf.ap[:, 0, :], A["mask"])
        t_mask = dve.do(op_tensor_copy, on(mask[:, :], maskf.ap[:, 0, :]), t)
        maskf.release(t_mask)
        upf, free = stage.take()
        st = stage_stream[(stage.at - 1) % 4]
        t = sp.dma(st, upf.ap[:, 0, :], A["upper"])
        t_up = dve.do(op_tensor_copy, on(upper[:, :], upf.ap[:, 0, :]), t)
        upf.release(t_up)

        def evac(out, in_, *toks):
            if dve.clock <= act.clock:
                return dve.do(op_tensor_copy, on(out, in_), *toks)
            return act.do(op_activation, on(out, in_, ACT.Copy), *toks)

        def turn(s, t, n, outs, rows=128):
            done = []
            for b0 in range(0, n, 4):
                k = min(4, n - b0)
                p, pf = ps.take()
                for j in range(k):
                    tt = pe.do(op_transpose, on(p.ap[:, j * 128:j * 128 + rows],
                                                          s.ap[0:rows, b0 + j, :], ident[0:rows, 0:rows]),
                               t, t_c, *pf, sig=(j == k - 1))
                    pf = []
                ts = []
                for o, i in outs(b0, k, p.ap):
                    if ts:
                        ts = [dve.do(op_tensor_copy, on(o, i), tt, ts)]
                    else:
                        ts = [evac(o, i, tt)]
                p.release(*ts)
                done += ts
                last = tt
            s.release(last)
            return done

        def v3(ap, k):
            return ap[:, 0:k * 128].rearrange("p (a n) -> p a n", a=k)

        W = {}

        def setup_a():
            s, t = staged([(lambda a: a[:, 0:3, :], A["L0_attn_w_in"].rearrange("(a p) d -> p a d", p=128)),
                           (lambda a: a[:, 3, :], A["L0_attn_w_out"])])
            W["a"] = turn(s, t, 4, lambda b0, k, p: [
                (winT[:, 0:256].rearrange("p (j d h) -> p j h d", j=2, d=8),
                 p[:, 0:256].rearrange("p (j h d) -> p j h d", j=2, d=8)),
                (winT[:, 256:384], p[:, 256:384]), (woutT[:, :], p[:, 384:512])])
            yield [ps]
            for name, dst, dj in (("L0_xattn_wk", wkT, wkJ), ("L0_xattn_wq", wqT, wqJ)):
                src = A[name].rearrange("(t h f e) d -> h e f t d", t=8, h=2, e=2)
                s, t = staged([(lambda a, q=2 * h + e: a[32 * q:32 * q + 32, :, :], src[h, e])
                               for h in range(2) for e in range(2)])

                def outs(b0, k, p, dst=dst, dj=dj):
                    pv = v3(p, 4)
                    o = [(dst[:, b0:b0 + 4, :], pv)]
                    for q in range(2):
                        o.append((dj[:, b0:b0 + 4, :].rearrange("p t (h e f) -> p t h e f", h=2, e=2)[:, :, :, q, :],
                                  pv.rearrange("p t (h e f) -> p t h e f", h=2, e=2)[:, :, :, 1 - q, :]))
                    return o
                W[name] = turn(s, t, 8, outs)
                yield [ps]
            s, t = staged([(lambda a: a[:, :, :], A["L0_xattn_wv"].rearrange("(t p) d -> p t d", p=128))])
            W["wv"] = turn(s, t, 8, lambda b0, k, p: [(wvT[:, b0:b0 + 4, :], v3(p, 4))])
            yield [ps]
            s, t = staged([(lambda a: a[:, :, :], A["L0_xattn_wo"].rearrange("o (t p) -> o t p", p=128))])
            W["wo"] = turn(s, t, 8, lambda b0, k, p: [(woT[:, b0:b0 + 4, :], v3(p, 4))])
            yield [ps]

        def setup_f():
            s, t = staged([(lambda a: a[0:8, 0, :], A["L0_ffn_router"])])
            W["rt"] = turn(s, t, 1, lambda b0, k, p: [(rtT[:, :], p[:, 0:8])], rows=8)
            yield [ps]
            W["f"] = []
            for half in range(2):
                for q, name in ((0, "L0_ffn_gate"), (1, "L0_ffn_up")):
                    src = A[name][4 * half:4 * half + 4].rearrange("e (t p) c -> p (e t) c", p=128)
                    s, t = staged([(lambda a: a[:, :, :], src)])
                    W["f"] += turn(s, t, 8, lambda b0, k, p, q=q, half=half: [
                        (wgu[:, 4 * half + b0 // 2:4 * half + b0 // 2 + 2, 256 * q:256 * q + 256],
                         p[:, :].rearrange("p (e n) -> p e n", e=2))])
                    yield [ps]
                src = A["L0_ffn_down"][4 * half:4 * half + 4].rearrange("e c (t h) -> c e t h", t=2)
                s, t = staged([(lambda a: a[:, :, :].rearrange("p (e t) h -> p e t h", t=2), src)])
                W["f"] += turn(s, t, 8, lambda b0, k, p, half=half: [
                    (wd[:, 4 * half + b0 // 2:4 * half + b0 // 2 + 2, :, :].rearrange("p e t n -> p (e t) n"), v3(p, 4))])
                yield [ps]
            s, t = staged([(lambda a: a[:, 0:2, :], A["L0_ffn_w_gate_s"].rearrange("(t p) c -> p t c", p=128)),
                           (lambda a: a[:, 2:4, :], A["L0_ffn_w_up_s"].rearrange("(t p) c -> p t c", p=128)),
                           (lambda a: a[:, 4:6, :], A["L0_ffn_w_down_s"].rearrange("c (t h) -> c t h", t=2))])

            def outs(b0, k, p):
                if b0 == 0:
                    return [(wgu[:, NE, :], p[:, :])]
                return [(wd[:, NE, :, :], v3(p, 2))]
            W["f"] += turn(s, t, 6, outs)
            yield ()

        xs = Ring([sb(f"x{i}", [128, 128]) for i in range(3)])
        d_x = [stream(f"d_x{i}") for i in range(3)]
        cs = Ring([sb(f"cx{i}", [128, 128]) for i in range(2)])
        d_cx = [stream(f"d_cx{i}") for i in range(2)]
        xab = Ring([sb(f"xab{i}", [128, 128]) for i in range(5)])
        arow = Ring([sb(f"arow{i}", [128, 128]) for i in range(2)])
        aT = Ring([sb(f"aT{i}", [128, 128]) for i in range(2)])
        qk = Ring([sb(f"qk{i}", [128, 2, 128]) for i in range(2)])
        res = Ring([sb(f"res{i}", [128, 2, 128]) for i in range(2)])
        parts = Ring([sb(f"parts{i}", [128, 2, 3, 128], BF16) for i in range(2)])
        d_sk = [stream(f"d_sk{i}") for i in range(3)]
        d_nm = [stream(f"d_nm{i}") for i in range(2)]
        d_zs = [stream(f"d_zs{i}") for i in range(2)]
        d_zn = [stream(f"d_zn{i}") for i in range(2)]
        vpad = Ring([sb(f"vpad{i}", [128, NH, 32]) for i in range(3)])
        QS = Ring([sb(f"QS{i}", [75, NH, 128], BF16) for i in range(3)])
        KS = [sb(f"KS{i}", [75, NH, 128], BF16) for i in range(3)]
        nm = Ring([sb(f"nm{i}", [128, 3, NH], BF16) for i in range(2)])
        nmf = [sb(f"nmf{i}", [128, 2, NH]) for i in range(2)]
        nmT = [sb(f"nmT{i}", [48, 128], BF16) for i in range(2)]
        PS = Ring([sb(f"PS{i}", [128, 4, 128]) for i in range(4)])
        oT = Ring([sb(f"oT{i}", [128, 512]) for i in range(2)])
        rs = Ring([sb(f"rs{i}", [128, NH]) for i in range(2)])
        cn = Ring([sb(f"cn{i}", [128, 128]) for i in range(2)])
        cnT = Ring([sb(f"cnT{i}", [128, 128]) for i in range(2)])
        x1 = Ring([sb(f"xi{i}", [128, 128]) for i in range(5)])
        lnr = Ring([sb(f"lnr{i}", [128, 128]) for i in range(3)])
        cT = Ring([sb(f"cT{i}", [128, 128]) for i in range(3)])
        cxT = Ring([sb(f"cxT{i}", [128, 128]) for i in range(2)])
        t12 = Ring([sb(f"t12_{i}", [128, 4, 128]) for i in range(2)])
        rot = Ring([sb(f"rot{i}", [128, 2, 8, 128]) for i in range(2)])
        V = Ring([sb(f"V{i}", [128, NH, 64]) for i in range(2)])
        mxs = Ring([sb(f"mxs{i}", [128, 16]) for i in range(2)])
        mx = Ring([sb(f"mx{i}", [128, 16]) for i in range(8)])
        PX = Ring([sb(f"PX{i}", [128, 4, 128]) for i in range(3)])
        PT = Ring([sb(f"PT{i}", [128, 4, 128]) for i in range(3)])
        oX = Ring([sb(f"oX{i}", [128, 4, 128]) for i in range(2)])
        erow = Ring([sb(f"er{i}", [128, 128]) for i in range(3)])
        d_er = [stream(f"d_er{i}") for i in range(3)]
        rows = Ring([sb(f"rows{i}", [128, 128]) for i in range(9)])
        d_rows = [stream(f"d_rows{i}") for i in range(9)]
        d_sc = [stream(f"d_sc{i}") for i in range(9)]
        d_yg = [stream(f"d_yg{i}") for i in range(9)]
        yst = Ring([sb(f"yst{i}", [128, 128]) for i in range(3)])
        d_yst = [stream(f"d_yst{i}") for i in range(3)]
        xsT = Ring([sb(f"xsT{i}", [128, 128]) for i in range(2)])
        cnt = sb("cnt", [128, 48])
        cmpb = sb("cmpb", [128, 256])
        posf = sb("posf", [128, 9 * 20])
        exf = sb("exf", [128, 32])
        eT = Ring([sb(f"eT{i}", [128, 128]) for i in range(2)])
        st6 = Ring([sb(f"st6_{i}", [128, 12]) for i in range(6)])
        lg = Ring([sb(f"lg{i}", [128, 40]) for i in range(2)])
        lgu = [sb(f"lgu{i}", [128, 8], U32) for i in range(2)]
        th = Ring([sb(f"th{i}", [128, 2, 256]) for i in range(2)])
        hb = Ring([sb(f"hb{i}", [128, 2, 128]) for i in range(3)])
        hT = Ring([sb(f"hT{i}", [128, 2, 128]) for i in range(2)])
        xo = Ring([sb(f"xo{i}", [128, 128]) for i in range(2)])
        d_o = [stream(f"d_o{i}") for i in range(2)]

        t_vp = []
        for s in vpad.slots:
            a = pool.do(op_memset, on(s.ap[:, :, :], 0.0))
            t_vp.append(pool.do(op_memset, on(s.ap[:, :, 8:9], 1.0), a))
        t_ks = [pool.do(op_memset, on(k[:, :, :], 1.0)) for k in KS]
        t_ks = t_ks[-1]

        loads = {}

        def load(b, key, ring, st, name):
            s, free = ring.take()
            i = s.i
            loads[key, b] = (s, sp.dma(st[i], s.ap[:, :], A[name][b], *free))

        def norm(x_ap, out, *toks):
            s, free = st6.take()
            a = dve.do(op_bn_stats, on(s.ap[:, 0:6], x_ap), *toks, *free)
            a = dve.do(op_bn_aggr, on(s.ap[:, 6:8], s.ap[:, 0:6]), a)
            a = dve.do(op_tensor_scalar, on(s.ap[:, 8:9], s.ap[:, 7:8], 1e-5, None, ALU.add), a)
            a = pool.do(op_tensor_tensor, on(s.ap[:, 9:10], s.ap[:, 8:9], nhalf[:, :], ALU.pow), a, t_nh)
            yield a
            o, free = out
            a = dve.do(op_tensor_scalar, on(o, x_ap, s.ap[:, 6:7], s.ap[:, 9:10], ALU.subtract, ALU.mult),
                       a, *free)
            s.release(a)
            return a

        def transp(src, dst, toks, ring):
            p, pf = ring.take()
            a = pe.do(op_transpose, on(p.ap[:, 0:128], src, ident[:, :]), *toks, *pf)
            d, df = dst
            c = evac(d, p.ap[:, 0:128], a, *df)
            p.release(c)
            return a, c

        ST = {}
        passed = set()

        def stage_a(b):
            if b + 1 < NB:
                load(b + 1, "x", xs, d_x, "x")
            x, tx = loads["x", b]
            yield tx
            ar, af = arow.take()
            ta = yield from norm(x.ap[:, :], (ar.ap[:, :], af), tx)
            xa, xf = xab.take()
            t1 = pool.do(op_tensor_tensor, on(xa.ap[:, :], x.ap[:, :], ar.ap[:, :], ALU.add), ta, *xf)
            t2 = pool.do(op_tensor_tensor, on(xa.ap[:, :], xa.ap[:, :], bo[:, :], ALU.add), t1, t_c)
            x.release(t1)
            yield [ta, ps]
            at, atf = aT.take()
            tp, tc = transp(ar.ap[:, :], (at.ap[:, :], atf), [ta], ps)
            ar.release(tp, t1)
            yield [tc, ps]
            p, pf = ps.take()
            pe.do(op_matmul, on(p.ap[:, 0:128], winT[:, 0:128], at.ap[:, :], start=True, stop=True),
                  tc, W["a"], *pf, sig=False)
            pe.do(op_matmul, on(p.ap[:, 128:256], winT[:, 128:256], at.ap[:, :], start=True, stop=True), sig=False)
            tm = pe.do(op_matmul, on(p.ap[:, 256:384], at.ap[:, :], winT[:, 256:384], start=True, stop=True))
            at.release(tm)
            q, qf = qk.take()
            tq = []
            for j in range(2):
                tq.append(act.do(op_activation, on(q.ap[:, j, :], p.ap[:, j * 128:j * 128 + 128],
                                                             ACT.Identity, bias=bqk[:, j:j + 1]), tm, t_c, *qf))
            vp, vf = vpad.take()
            tv = dve.do(op_tensor_tensor, on(vp.ap[:, :, 0:8],
                                                  p.ap[:, 256:384].rearrange("p (h d) -> p h d", h=NH),
                                                  bv[:, :].rearrange("p (h d) -> p h d", h=NH), ALU.add),
                        tm, t_c, tq[1], *t_vp, *vf)
            p.release(tq[1], tv)
            pt, ptf = parts.take()
            r, rf = res.take()
            passed.add(("a", b))
            yield tq
            a = act.do(op_activation, on(pt.ap[:, :, 0, :], q.ap[:, :, :], ACT.Copy), *tq, *ptf)
            a = pool.do(op_tensor_tensor, on(r.ap[:, :, :], q.ap[:, :, :], pt.ap[:, :, 0, :], ALU.subtract), a, *rf)
            q.release(a)
            yield a
            a = act.do(op_activation, on(pt.ap[:, :, 1, :], r.ap[:, :, :], ACT.Copy), a)
            a = pool.do(op_tensor_tensor, on(pt.ap[:, :, 2, :], r.ap[:, :, :], pt.ap[:, :, 1, :], ALU.subtract), a)
            r.release(a)
            yield a
            Q, Qf = QS.take()
            i = Q.i
            K = KS[i]
            Z = A["z_qk"]
            ts = sp.dma(d_zs[b % 2], Z[b].rearrange("j m p t -> p j m t"), pt.ap[:, :, :, :], a)
            for g in range(3):
                for m in range(3):
                    sp.dma(d_sk[i], Q.ap[24 * g + 8 * m:24 * g + 8 * m + 8, :, :],
                           Z[b, 0, g].rearrange("(d h) t -> d h t", d=8), ts, *Qf)
                td = sp.dma(d_sk[i], K[24 * g:24 * g + 24, :, :],
                            Z[b, 1].rearrange("m (d h) t -> (m d) h t", d=8), ts, t_ks, *Qf)
            pt.release(ts)
            ST["A", b] = (xa, t2, vp, tv, Q, K, td)

        def stage_b1(b):
            xa, t2, vp, tv, Q, K, td = ST["A", b]
            yield [td, ps]
            m, mf = mxs.take()
            for g in range(4):
                p, pf = ps.take()
                for c in range(4):
                    h = 4 * g + c
                    t = pe.do(op_matmul, on(p.ap[:, c * 128:c * 128 + 128], Q.ap[0:72, h, :],
                                                           K[0:72, h, :], start=True, stop=True),
                              td, *pf, sig=(c == 3))
                    pf = []
                yield t
                t = dve.do(op_tensor_reduce, on(m.ap[:, 4 * g:4 * g + 4],
                                                          p.ap.rearrange("p (h k) -> p h k", h=4), AX.X, ALU.max),
                           t, *mf)
                p.release(t)
                yield [ps]
            n, nf = nm.take()
            f = nmf[b % 2]
            a = dve.do(op_tensor_scalar, on(f[:, 0, :], m.ap[:, :], -1.0, None, ALU.mult), t, *nf)
            m.release(a)
            a = dve.do(op_tensor_copy, on(n.ap[:, 0, :], f[:, 0, :]), a)
            a = dve.do(op_tensor_tensor, on(f[:, 1, :], f[:, 0, :], n.ap[:, 0, :], ALU.subtract), a)
            a = dve.do(op_tensor_copy, on(n.ap[:, 1, :], f[:, 1, :]), a)
            a = dve.do(op_tensor_tensor, on(n.ap[:, 2, :], f[:, 1, :], n.ap[:, 1, :], ALU.subtract), a)
            yield [a, ps]
            p, pf = ps.take()
            pb = p.ap[0:48, 0:64].bitcast(BF16)
            a = pe.do(op_transpose, on(pb, n.ap[:, :, :].rearrange("p a h -> p (a h)"), identb[:, :]),
                      a, t_idb, *pf)
            c = act.do(op_activation, on(nmT[b % 2][:, :], pb, ACT.Copy), a, ST.get(("nmT", b % 2)))
            p.release(c)
            n.release(a)
            t = sp.dma(d_zn[b % 2], A["z_nm"][b], nmT[b % 2][:, :], c)
            tn = sp.dma(d_nm[b % 2], Q.ap[72:75, :, :], A["z_nm"][b].rearrange("(j h) t -> j h t", j=3), t)
            ST["nmT", b % 2] = t
            ST["B1", b] = tn

        def stage_b2(b):
            xa, t2, vp, tv, Q, K, td = ST["A", b]
            tn = ST["B1", b]
            yield [tn, ps]
            prev = []
            for g in range(4):
                p, pf = ps.take()
                for c in range(4):
                    h = 4 * g + c
                    t = pe.do(op_matmul, on(p.ap[:, c * 128:c * 128 + 128], K[0:75, h, :], Q.ap[0:75, h, :],
                                            start=True, stop=True), tn, *pf, sig=(c == 3))
                if g == 3:
                    Q.release(t)
                yield t
                s, sf = PS.take()
                te = act.do(op_activation, on(s.ap[:, :, :].rearrange("p h q -> p (h q)"), p.ap, ACT.Exp,
                                              scale=S_SELF), t, *sf)
                p.release(te)
                prev.append((s, te))
                yield [te, ps] if g == 3 else [ps]
            o, of = ps.take()
            for g in range(4):
                s, te = prev[g]
                for c in range(4):
                    h = 4 * g + c
                    tp = pe.do(op_matmul, on(o.ap[32 * c:32 * c + 32, g * 128:(g + 1) * 128], vp.ap[:, h, :],
                                             s.ap[:, c, :], start=True, stop=True), te, tv, *of, sig=(c == 3))
                s.release(tp)
            vp.release(tp)
            ot, otf = oT.take()
            c = evac(ot.ap[:, :], o.ap, tp, *otf)
            o.release(c)
            passed.add(("b2", b))
            yield [c, ps]
            p, pf = ps.take()
            for g in range(4):
                t = pe.do(op_transpose, on(p.ap[:, g * 128:g * 128 + 128], ot.ap[:, g * 128:g * 128 + 128],
                                                     ident[:, :]), c, *pf, sig=(g == 3))
                pf = []
            ot.release(t)
            pv = p.ap.rearrange("p (h d) -> p h d", h=NH)
            r, rf = rs.take()
            a = dve.do(op_reciprocal, on(r.ap[:, :].rearrange("p (h a) -> p h a", a=1), pv[:, :, 8:9]), t, *rf)
            n, nf = cn.take()
            a = dve.do(op_tensor_tensor, on(n.ap[:, :].rearrange("p (h d) -> p h d", h=NH), pv[:, :, 0:8],
                                                 r.ap[:, :].rearrange("p (h a) -> p h a", a=1).to_broadcast([128, NH, 8]),
                                                 ALU.mult), a, *nf)
            p.release(a)
            r.release(a)
            yield [a, ps]
            nt, ntf = cnT.take()
            tp, c = transp(n.ap[:, :], (nt.ap[:, :], ntf), [a], ps)
            n.release(tp)
            yield [c, ps]
            p, pf = ps.take()
            t = pe.do(op_matmul, on(p.ap[:, 0:128], nt.ap[:, :], woutT[:, :], start=True, stop=True), c, *pf)
            nt.release(t)
            x, xf = x1.take()
            a = dve.do(op_tensor_tensor, on(x.ap[:, :], p.ap[:, 0:128], xa.ap[:, :], ALU.add), t, t2, *xf)
            p.release(a)
            xa.release(a)
            yield a
            l, lf = lnr.take()
            tl = yield from norm(x.ap[:, :], (l.ap[:, :], lf), a)
            yield [tl, ps]
            ct, cf = cT.take()
            tp, c = transp(l.ap[:, :], (ct.ap[:, :], cf), [tl], ps)
            l.release(tp)
            ST["B", b] = (x, a, ct, c)

        def stage_c(b):
            if b + 1 < NB:
                load(b + 1, "c", cs, d_cx, "ctx_1024")
            cx, tcx = loads["c", b]
            yield [tcx, ps]
            xt, xf = cxT.take()
            tp, tk = transp(cx.ap[:, :], (xt.ap[:, :], xf), [tcx, t_c], ps)
            cx.release(tp)
            yield [tk, ps]
            ST["cx", b] = (xt, tk)
            v, vf = V.take()
            tv = []
            for half in range(2):
                p, pf = ps.take()
                t = pe.do(op_matmul, on(p.ap, xt.ap[:, :],
                                             wvT[:, 4 * half:4 * half + 4, :].rearrange("p a n -> p (a n)"),
                                             start=True, stop=True), tk, W["wv"], *pf)
                yield t
                c = evac(v.ap[:, 8 * half:8 * half + 8, :].rearrange("p h d -> p (h d)"), p.ap, t, *vf)
                p.release(c)
                tv.append(c)
                yield [ps]
            ST["C", b] = (v, tv, t)

        def stage_r(i):
            b, j, half = i // 4, 1 - i % 4 // 2, i % 2
            if j:
                src, ts = ST["cx", b]
                w, wj, name = wkT, wkJ, "L0_xattn_wk"
            else:
                _, _, src, ts = ST["B", b]
                w, wj, name = wqT, wqJ, "L0_xattn_wq"
            yield [ts, ps, rot] if i % 4 == 0 else [ts, ps]
            if i % 4 == 0:
                ST["rot", b] = (*rot.take(), [])
            R, Rf, tr = ST["rot", b]
            p, pf = ps.take()
            for c in range(4):
                t = pe.do(op_matmul, on(p.ap[:, c * 128:c * 128 + 128], w[:, 4 * half + c, :],
                                        src.ap[:, :], start=True, stop=True),
                          ts, W[name], *pf, sig=(c == 3))
            r = R.ap[:, j, 4 * half:4 * half + 4, :]
            p3 = p.ap.rearrange("p (c t) -> p c t", c=4)
            cos3, sin3 = (w[:, :].rearrange("p (a t) -> p a t", a=1).to_broadcast([128, 4, 128]) for w in (cos, sin))
            yield [t, ps]
            a1 = dve.do(op_tensor_tensor, on(r, p3, cos3, ALU.mult), t, *Rf)
            p.release(a1)
            p, pf = ps.take()
            for c in range(4):
                t = pe.do(op_matmul, on(p.ap[:, c * 128:c * 128 + 128], wj[:, 4 * half + c, :],
                                        src.ap[:, :], start=True, stop=True),
                          ts, W[name], *pf, sig=(c == 3))
            if half == 1:
                src.release(t, ST["C", b][2] if j else None)
            passed.add(("r", i))
            yield [t, t12]
            T, Tf = t12.take()
            t = dve.do(op_tensor_tensor, on(T.ap[:, :, :], p.ap.rearrange("p (c t) -> p c t", c=4), sin3, ALU.mult),
                       t, *Tf)
            p.release(t)
            yield [t, a1]
            t = pool.do(op_tensor_tensor, on(r, r, T.ap[:, :, :], ALU.add), t, a1)
            T.release(t)
            tr.append(t)

        def stage_d(b):
            v, tv, _ = ST["C", b]
            R, _, tr = ST["rot", b]
            x, tx1, _, _ = ST["B", b]
            yield [tr, ps]
            m, mf = mx.take()
            nb, nbf = mx.take()
            sm, smf = mx.take()
            ri, rif = mx.take()
            hist = {}
            outs = []
            for g in range(7):
                if g < 4:
                    p, pf = ps.take()
                    pe.do(op_matmul, on(p.ap.rearrange("p (c k) -> p c k", c=4), identb[:, :],
                                        mask[:, :].rearrange("p (a k) -> p a k", a=1).to_broadcast([128, 4, 128]),
                                        start=True, stop=False,
                                        skip_group_check=True), t_idb, t_mask, *pf, sig=False)
                    for c in range(4):
                        q = 4 * (g // 2) + c
                        lo = 64 * (g % 2)
                        t = pe.do(op_matmul, on(p.ap[:, c * 128:c * 128 + 128], R.ap[lo:lo + 64, 0, q, :],
                                                R.ap[lo:lo + 64, 1, q, :], start=False, stop=(c == 3),
                                                skip_group_check=True), tr, sig=(c == 3))
                    if g == 3:
                        R.release(t)
                yield [t, ps, oX] if g in (4, 6) else t
                if g < 4:
                    t = dve.do(op_tensor_reduce, on(m.ap[:, 4 * g:4 * g + 4],
                                                    p.ap.rearrange("p (h k) -> p h k", h=4), AX.X, ALU.max), t, *mf)
                    t = dve.do(op_tensor_scalar, on(nb.ap[:, 4 * g:4 * g + 4], m.ap[:, 4 * g:4 * g + 4], -S_X, None,
                                                    ALU.mult), t, *nbf)
                if 3 <= g and (g - 3) % 2:
                    k = g - 3
                    o, of = ps.take()
                    for c in range(4):
                        for u in range(2):
                            pt, to = hist[k - 1 + u]
                            h = 4 * (k - 1) + 2 * c + u
                            tp = pe.do(op_matmul, on(o.ap[64 * u:64 * u + 64, c * 128:c * 128 + 128], v.ap[:, h, :],
                                                     pt.ap[:, c, :], start=True, stop=True), to, tv, *of,
                                       sig=(c == 3 and u == 1))
                    hist[k][0].release(tp)
                    hist[k - 1][0].release(tp)
                    ox, oxf = oX.take()
                    to = evac(ox.ap[:, :, :].rearrange("p h q -> p (h q)"), o.ap, tp, *oxf)
                    o.release(to)
                    outs.append((ox, to))
                yield [t, hist[g - 2][1], ps, PT] if 2 <= g < 6 else t
                if g < 4:
                    e_, ef = PX.take()
                    for c in range(4):
                        h = 4 * g + c
                        te = act.do(op_activation, on(e_.ap[:, c, :], p.ap[:, c * 128:c * 128 + 128], ACT.Exp,
                                                      bias=nb.ap[:, h:h + 1], scale=S_X, accum_out=sm.ap[:, h:h + 1]),
                                    t, *ef, *smf)
                    p.release(te)
                    hist[g] = [e_, te]
                if 1 <= g < 5:
                    k = g - 1
                    e_, t1 = hist[k]
                    t1 = dve.do(op_reciprocal, on(ri.ap[:, 4 * k:4 * k + 4], sm.ap[:, 4 * k:4 * k + 4]), t1, *rif)
                    t1 = pool.do(op_tensor_tensor, on(
                        e_.ap[:, :, :], e_.ap[:, :, :],
                        ri.ap[:, 4 * k:4 * k + 4].rearrange("p (h a) -> p h a", a=1).to_broadcast([128, 4, 128]),
                        ALU.mult), t1)
                    hist[k] = [e_, t1]
                if 2 <= g < 6:
                    n, tn = hist[g - 2]
                    pp, pf = ps.take()
                    for c in range(4):
                        tn = pe.do(op_transpose, on(pp.ap[:, c * 128:c * 128 + 128], n.ap[:, c, :], ident[:, :]),
                                   tn, *pf, sig=(c == 3))
                    n.release(tn)
                    pt, ptf = PT.take()
                    tt = evac(pt.ap[:, :, :].rearrange("p h q -> p (h q)"), pp.ap, tn, *ptf)
                    pp.release(tt)
                    hist[g - 2] = [pt, tt]
                if g == 4:
                    passed.add(("d", b))
                yield [ps] if g < 3 else ()
            for s in (m, nb, sm, ri):
                s.release(te, tn)
            v.release(tp)
            yield [[t for _, t in outs], ps]
            p, pf = ps.take()
            for q in range(8):
                ox, to = outs[q // 4]
                t = pe.do(op_matmul, on(p.ap[:, 0:128], ox.ap[:, q % 4, :], woT[:, q, :],
                                                         start=(q == 0), stop=(q == 7)),
                          to, W["wo"], *pf, sig=(q == 7))
                pf = []
            for ox, _ in outs:
                ox.release(t)
            y = xsum[:, b, :]
            a = dve.do(op_tensor_tensor, on(y, p.ap[:, 0:128], x.ap[:, :], ALU.add), t, tx1,
                       [q for s in stage.slots for q in s.free])
            p.release(a)
            x.release(a)
            ST["D", b] = (y, a)

        def stage_e(b):
            y, a = ST["D", b]
            yield a
            l, lf = erow.take()
            i = l.i
            tl = yield from norm(y, (l.ap[:, :], lf), a)
            tz = sp.dma(d_er[i], A["z_e"][b], l.ap[:, :], tl)
            yield [tl, ps]
            et, ef = eT.take()
            tp, c = transp(l.ap[:, :], (et.ap[:, :], ef), [tl], ps)
            l.release(tp, tz)
            ST["ze", b] = tz
            ST["E", b] = (y, a, et, c)

        def gated(p, T, Tf, H, Hf, t):
            t = act.do(op_activation, on(T.ap[:, 0, :], p.ap[:, 0:256], ACT.Tanh, scale=0.5), t, *Tf)
            t = dve.do(op_scalar_tensor_tensor, on(out=T.ap[:, 1, :], in0=T.ap[:, 0, :], scalar=1.0,
                                                   in1=p.ap[:, 0:256], op0=ALU.add, op1=ALU.mult), t)
            t = dve.do(op_scalar_tensor_tensor, on(out=H.ap[:, :, :].rearrange("p a n -> p (a n)"), in0=T.ap[:, 1, :],
                                                   scalar=0.5, in1=p.ap[:, 256:512], op0=ALU.mult, op1=ALU.mult),
                       t, *Hf)
            p.release(t)
            T.release(t)
            return t

        def stage_f(b):
            y, ty, et, te = ST["E", b]
            yield [te, ps]
            p, pf = ps.take()
            t = pe.do(op_matmul, on(p.ap[:, 0:8], et.ap[:, :], rtT[:, :], start=True, stop=True), te, W["rt"], *pf)
            L, Lf = lg.take()
            U = lgu[b % 2]
            a = dve.do(op_tensor_copy, on(L.ap[:, 0:8], p.ap[:, 0:8]), t, *Lf)
            p.release(a)
            a = dve.do(op_max, on(L.ap[:, 8:16], L.ap[:, 0:8]), a)
            a = dve.do(op_max_index, on(U[:, :], L.ap[:, 8:16], L.ap[:, 0:8]), a)
            a = dve.do(op_tensor_copy, on(L.ap[:, 16:17], U[:, 0:1]), a)
            a = dve.do(op_tensor_scalar, on(OH[:, b, :], iota[:, :], L.ap[:, 16:17], None, ALU.is_equal), a)
            L.release(a)
            ST["OH", b] = a
            yield [ps, hb]
            p, pf = ps.take()
            for c in range(4):
                t = pe.do(op_matmul, on(p.ap[:, 128 * c:128 * c + 128], wgu[:, NE, 128 * c:128 * c + 128], et.ap[:, :],
                                        start=True, stop=True), te, W["f"], *pf, sig=(c == 3))
            et.release(t)
            T, Tf = th.take()
            H, Hf = hb.take()
            t = gated(p, T, Tf, H, Hf, t)
            yield [t, ps]
            p, pf = ps.take()
            for c in range(2):
                t = pe.do(op_matmul, on(p.ap[:, 0:128], H.ap[:, c, :], wd[:, NE, c, :], start=(c == 0), stop=(c == 1)),
                          t, *pf, sig=(c == 1))
            H.release(t)
            t = dve.do(op_tensor_tensor, on(y, p.ap[:, 0:128], y, ALU.add), t, ty)
            p.release(t)
            ST["F", b] = t

        wguf = wgu[:, 0:NE, :].rearrange("p e n -> p (e n)")
        wdf = wd[:, 0:NE, :, :].rearrange("p e t n -> p (e t n)")

        def dispatch(k):
            n, T = CHUNKS[k], TILES[k]
            b0, t0 = sum(CHUNKS[:k]), sum(TILES[:k])
            toh = [ST["OH", b0 + n - 1]]
            p, pf = ps.take()
            t = pe.do(op_matmul, on(p.ap[:, 0:8 * n], upper[:, :], OH[:, b0:b0 + n, :].rearrange("p b e -> p (b e)"),
                                    start=True, stop=False, skip_group_check=True), toh, t_up, t_on, *pf, sig=False)
            for i in range(n - 1):
                t = pe.do(op_matmul, on(p.ap[:, 8 * i + 8:8 * n].rearrange("p (b e) -> p b e", e=NE), ones[:, :],
                                        OH[:, b0 + i:b0 + i + 1, :].to_broadcast([128, n - 1 - i, NE]),
                                        start=False, stop=False, skip_group_check=True), sig=False)
            for i in range(n):
                pe.do(op_matmul, on(p.ap[:, 8 * n:8 * n + 8], ones[:, :], OH[:, b0 + i, :], start=False, stop=False,
                                    skip_group_check=True), sig=False)
            t = pe.do(op_matmul, on(p.ap[:, 0:8 * n + 8], identb[:, :], zero[:, :].bitcast(BF16)[:, 0:8 * n + 8],
                                    start=False, stop=True, skip_group_check=True), t_z)
            a = dve.do(op_tensor_copy, on(cnt[:, 0:8], p.ap[:, 8 * n:8 * n + 8]), t, ST.get("disp"))
            cm = cmpb[:, 0:8 * n].rearrange("p (e j) -> p e j", e=NE)
            a = dve.do(op_tensor_tensor, on(cm, cnt[:, 0:8].rearrange("p (e a) -> p e a", a=1).to_broadcast([128, NE, n]),
                                            steps[:, 0:n].rearrange("p (a j) -> p a j", a=1).to_broadcast([128, NE, n]),
                                            ALU.is_gt), a, t_c)
            a = dve.do(op_tensor_reduce, on(cnt[:, 8:16], cm, AX.X, ALU.add), a)
            c2 = cmpb[:, 0:64].rearrange("p (e f) -> p e f", e=NE)
            a = dve.do(op_tensor_tensor, on(c2, cnt[:, 8:16].rearrange("p (a f) -> p a f", a=1).to_broadcast([128, NE, NE]),
                                            tri[:, :, :], ALU.mult), a)
            a = dve.do(op_tensor_reduce, on(cnt[:, 16:24], c2, AX.X, ALU.add), a)
            a = dve.do(op_tensor_scalar, on(cnt[:, 24:32], cnt[:, 16:24], 128.0, None, ALU.mult), a)
            a = dve.do(op_tensor_tensor, on(cnt[:, 32:40], cnt[:, 16:24], cnt[:, 8:16], ALU.add), a)
            a = dve.do(op_tensor_scalar, on(cnt[:, 40:48], cnt[:, 32:40], 128.0, None, ALU.mult), a)
            pv = posf[:, 0:8 * n].rearrange("p (b e) -> p b e", e=NE)
            d = dve.do(op_tensor_tensor, on(pv, p.ap[:, 0:8 * n].rearrange("p (b e) -> p b e", e=NE),
                                            cnt[:, 24:32].rearrange("p (a e) -> p a e", a=1).to_broadcast([128, n, NE]),
                                            ALU.add), a, t)
            p.release(d)
            d = dve.do(op_tensor_tensor, on(pv, pv, OH[:, b0:b0 + n, :], ALU.mult), d)
            d = dve.do(op_tensor_reduce, on(posf[:, 160:160 + n], pv, AX.X, ALU.add), d)
            d = dve.do(op_tensor_copy, on(pos[:, b0:b0 + n], posf[:, 160:160 + n]), d)
            yield ()
            c3 = cmpb[:, 0:8 * T].rearrange("p (j e) -> p j e", e=NE)
            a = dve.do(op_tensor_tensor, on(c3, cnt[:, 40:48].rearrange("p (a e) -> p a e", a=1).to_broadcast([128, T, NE]),
                                            steps[:, 0:T].rearrange("p (j a) -> p j a", a=1).to_broadcast([128, T, NE]),
                                            ALU.is_le), a, d)
            a = dve.do(op_tensor_reduce, on(exf[:, 0:T], c3, AX.X, ALU.add), a)
            a = dve.do(op_tensor_scalar, on(exf[:, 0:T], exf[:, 0:T], 7.0, None, ALU.min), a)
            a1 = dve.do(op_tensor_scalar, on(exg[:, t0:t0 + T], exf[:, 0:T], 512.0, None, ALU.mult), a)
            a2 = dve.do(op_tensor_scalar, on(exd[:, t0:t0 + T], exf[:, 0:T], 256.0, None, ALU.mult), a)
            ST["disp"] = a2
            ST["ex", k] = [a1, a2]
            ts, got = [], []
            for b in range(b0, b0 + n + 2):
                yield [rows]
                if b < b0 + n:
                    r, rf = rows.take()
                    got.append((b, r, sp.dma(d_rows[r.i], r.ap[:, :], A["z_e"][b], ST["ze", b], *rf)))
                if b >= b0 + 2:
                    c, r, tr = got.pop(0)
                    yield [tr, d]
                    t = pool.dma_by(op_scatter, d_sc[r.i], on(A["z_xs"][k], pos[:, c:c + 1], r.ap[:, :]), tr, d, t_zero)
                    r.release(t)
                    ts.append(t)
            ST["xs", k] = ts[-3:]
            ST["pos", k] = d

        def tile(k, j):
            r0 = 128 * (j - sum(TILES[:k]))
            yield [rows]
            x, xf = rows.take()
            i = x.i
            t = sp.dma(d_rows[i], x.ap[:, :], A["z_xs"][k][r0:r0 + 128, :], ST["xs", k], *xf)
            yield [t, ps, xsT]
            at = []
            pe.do(op_load_expert, on(at, exg[0:1, j:j + 1], exd[0:1, j:j + 1]), ST["ex", k], sig=False)
            xt, xtf = xsT.take()
            tp, t = transp(x.ap[:, :], (xt.ap[:, :], xtf), [t], ps)
            x.release(tp)
            yield [t, ps, hb, th]
            p, pf = ps.take()
            t = pe.do(op_matmul_expert, on(p.ap, xt.ap[:, :], wguf, at), t, *pf)
            xt.release(t)
            T, Tf = th.take()
            H, Hf = hb.take()
            t = gated(p, T, Tf, H, Hf, t)
            yield [t, ps, hT]
            p, pf = ps.take()
            for c in range(2):
                t = pe.do(op_transpose, on(p.ap[:, c * 128:c * 128 + 128], H.ap[:, c, :], ident[:, :]), t, *pf,
                          sig=(c == 1))
            H.release(t)
            G, Gf = hT.take()
            t = evac(G.ap[:, :, :].rearrange("p a n -> p (a n)"), p.ap[:, 0:256], t, *Gf)
            p.release(t)
            yield [t, ps, yst]
            p, pf = ps.take()
            t = pe.do(op_matmul_expert2, on(p.ap[:, 0:128], G.ap, wdf, at), t, *pf)
            G.release(t)
            y, yf = yst.take()
            i = y.i
            t = evac(y.ap[:, :], p.ap[:, 0:128], t, *yf)
            p.release(t)
            t = sp.dma(d_yst[i], A["z_ys"][k][r0:r0 + 128, :], y.ap[:, :], t)
            y.release(t)
            ST.setdefault(("ys", k), []).append(t)

        def collect(k):
            b0, n = sum(CHUNKS[:k]), CHUNKS[k]
            got = []
            for b in range(b0, b0 + n + 2):
                if b < b0 + n:
                    yield [rows, ST["ys", k][-3:]]
                    y, yf = rows.take()
                    got.append((b, y, pool.dma_by(op_gather, d_yg[y.i], on(y.ap[:, :], A["z_ys"][k], pos[:, b:b + 1]),
                                                  ST["pos", k], ST["ys", k][-3:], *yf)))
                if b >= b0 + 2:
                    c, y, t = got.pop(0)
                    yield t
                    o, of = xo.take()
                    a = dve.do(op_tensor_tensor, on(o.ap[:, :], y.ap[:, :], xsum[:, c, :], ALU.add), t, ST["F", c],
                               *of)
                    y.release(a)
                    o.release(sp.dma(d_o[o.i], A["out"][c], o.ap[:, :], a))


        load(0, "x", xs, d_x, "x")
        rest_a = setup_a()
        next(rest_a)

        load(0, "c", cs, d_cx, "ctx_1024")
        for k, n in enumerate(TILES):
            t_zero = sp.dma(d_zero, A["z_xs"][k].rearrange("(j p) d -> p j d", p=128),
                            zero[:, :].rearrange("p (a d) -> p a d", a=1).to_broadcast([128, n, 128]), t_z)

        jobs = {("setup_a", 0): (SETUP[0], lambda: rest_a, (), []), ("setup", 0): (SETUP[1], setup_f, (), [("setup_a", 0)])}
        for b in range(NB):
            jobs["A", b] = (b + LEAD["A"], stage_a, (b,), [("a", b - 1), ("b2", b - 3)])
            jobs["B1", b] = (b + LEAD["B1"], stage_b1, (b,), [("A", b), ("B1", b - 1)])
            jobs["B2", b] = (b + LEAD["B2"], stage_b2, (b,), [("B1", b), ("b2", b - 1), ("R", 4 * b - 9), ("D", b - 4)])
            jobs["C", b] = (b + LEAD["C"], stage_c, (b,), [("C", b - 1), ("r", 4 * b - 7), ("D", b - 2), ("setup_a", 0)])
            for i in range(4):
                jobs["R", 4 * b + i] = (b + LEAD["R"][i], stage_r, (4 * b + i,),
                                        [("B2" if i > 1 else "C", b), ("r", 4 * b + i - 1), ("d", b - 2), ("setup_a", 0)])
            jobs["D", b] = (b + LEAD["D"], stage_d, (b,), [("C", b), *(("R", 4 * b + i) for i in range(4)), ("d", b - 1),
                                                           ("setup", 0)])
            jobs["E", b] = (b + LEAD["E"], stage_e, (b,), [("D", b), ("E", b - 1), ("F", b - 2)])
            jobs["F", b] = (b + LEAD["F"], stage_f, (b,), [("E", b), ("F", b - 1)])
        for k, n in enumerate(CHUNKS):
            b0, t0, T = sum(CHUNKS[:k]), sum(TILES[:k]), TILES[k]
            jobs["dispatch", k] = (b0 + n, dispatch, (k,), [("F", b0 + n - 1), ("collect", k - 1)])
            for j in range(T):
                jobs["tile", t0 + j] = (b0 + n + LEAD["tile"] + LEAD["rate"] * j, tile, (k, t0 + j),
                                        [("dispatch", k), ("tile", t0 + j - DEPTH)])
            jobs["collect", k] = (b0 + n + 12, collect, (k,), [("tile", t0 + T - 1 - u) for u in range(DEPTH)])
        todo, live = list(jobs), []
        while todo or live:
            for j in list(todo):
                prio, f, args, before = jobs[j]
                if all(q[1] < 0 or q in passed for q in before):
                    live.append([(), prio, j, f(*args)])
                    todo.remove(j)
            live.sort(key=lambda v: (max(when([v[0]]) - pe.clock, 0), v[1], v[2]))
            v = live[0]
            assert when([v[0]]) < 1e9, [u[2] for u in live]
            try:
                v[0] = next(v[3])
            except StopIteration:
                live.pop(0)
                passed.add(v[2])
        for st in d_o:
            sp.wait((st[0], st[1], 0))

        block = ctx.enter_context(nc.Block())
        for name, q in (("sync", sp), ("tensor", pe), ("vector", dve), ("scalar", act), ("gpsimd", pool)):
            def body(eng, q=q):
                for op in q.ops:
                    op(eng)
            {"sync": block.sync, "tensor": block.tensor, "vector": block.vector, "scalar": block.scalar,
             "gpsimd": block.gpsimd}[name](body)


_INS = ['x', 'ctx_1024', 'L0_attn_w_in', 'L0_attn_b_in', 'L0_attn_w_out', 'L0_attn_b_out', 'L0_xattn_wq',
        'L0_xattn_wk', 'L0_xattn_wv', 'L0_xattn_wo', 'L0_ffn_up', 'L0_ffn_gate', 'L0_ffn_down', 'L0_ffn_router',
        'L0_ffn_w_up_s', 'L0_ffn_w_gate_s', 'L0_ffn_w_down_s']


def kernel(**inputs):
    import numpy as np
    import concourse.bacc as bacc
    from concourse.bass_utils import run_bass_kernel_spmd

    f = np.float32
    freqs = (f(1.0) / f(10000.0) ** (np.arange(0, 64, 2, dtype=f) / f(64))).astype(f)
    ang = np.arange(128, dtype=f)[:, None] * freqs[None, :]
    c, s = np.cos(ang).astype(f).T, np.sin(ang).astype(f).T
    i, j = np.arange(128)[:, None], np.arange(128)[None, :]
    band = np.where((j <= i) & (j >= i - 32), f(0), f(-1e30)).astype(f)
    arrays = {n: np.ascontiguousarray(inputs[n]) for n in _INS}
    arrays["ident"] = np.eye(128, dtype=f)
    arrays["cos"] = np.concatenate([c] * 4)
    arrays["sin"] = np.concatenate([-s, s, -s, s])
    arrays["mask"] = band
    arrays["iota"] = np.tile(np.arange(8, dtype=f), (128, 1))
    arrays["steps"] = np.tile(np.arange(32, dtype=f) * f(128), (128, 1))
    arrays["tri"] = np.tile(np.tril(np.ones((8, 8), f), -1).reshape(1, 64), (128, 1))
    arrays["upper"] = np.triu(np.ones((128, 128), f), 1)
    arrays["bqk"] = np.ascontiguousarray(
        arrays["L0_attn_b_in"][0:256].reshape(2, 16, 8).transpose(2, 1, 0).reshape(128, 2))
    arrays["bvb"] = np.ascontiguousarray(np.broadcast_to(arrays["L0_attn_b_in"][256:384], (128, 128)))
    arrays["bob"] = np.ascontiguousarray(np.broadcast_to(arrays["L0_attn_b_out"], (128, 128)))

    nc = bacc.Bacc("TRN2", target_bir_lowering=False, num_devices=1)
    A = {n: nc.dram_tensor(f"in_{n}", a.shape, mybir.dt.from_np(a.dtype), kind="ExternalInput").ap()
         for n, a in arrays.items()}
    A["out"] = nc.dram_tensor("out_0", (32, 128, 128), F32, kind="ExternalOutput").ap()
    A["z_qk"] = nc.dram_tensor("z_qk", (32, 2, 3, 128, 128), BF16, kind="Internal").ap()
    A["z_nm"] = nc.dram_tensor("z_nm", (32, 48, 128), BF16, kind="Internal").ap()
    A["z_e"] = nc.dram_tensor("z_e", (32, 128, 128), F32, kind="Internal").ap()
    A["z_xs"] = [nc.dram_tensor(f"z_xs{i}", (n * 128, 128), F32, kind="Internal").ap() for i, n in enumerate(TILES)]
    A["z_ys"] = [nc.dram_tensor(f"z_ys{i}", (n * 128, 128), F32, kind="Internal").ap() for i, n in enumerate(TILES)]
    build(nc, A)
    r = run_bass_kernel_spmd(nc, [{f"in_{n}": a for n, a in arrays.items()}], core_ids=[0])
    return r.results[0]["out_0"]
```
